# Optimizing a Trainium2 kernel written in Bass

```python
import numpy as np
import jax
import jax.numpy as jnp

def _softmax(x, axis=-1):
    return jax.nn.softmax(x, axis=axis)

def _gelu(x):
    return jax.nn.gelu(x, approximate=True)

def _silu(x):
    return jax.nn.silu(x)

def _sigmoid(x):
    return jax.nn.sigmoid(x)

def _layernorm(x, axis=-1, eps=1e-05):
    m = jnp.mean(x, axis=axis, keepdims=True)
    v = jnp.var(x, axis=axis, keepdims=True)
    return (x - m) / jnp.sqrt(v + eps)

def _scatter_add(tgt, idx, src, axis=0):
    return tgt.at[idx].add(src)

def _segment_sum(src, seg, n):
    return jax.ops.segment_sum(src, seg, n)
kernel_name = 'mk_decoder_postln_d4_seqx_r8_062022'

def setup_inputs(seed: int=0):
    np.random.seed(seed)
    _w = jnp.asarray

    def _rec_inputs():
        import jax
        import jax.numpy as jnp
        _rk = jax.random.key(seed)
        x = -0.0003929 + 0.9999 * jax.random.normal(jax.random.fold_in(_rk, 1), (32, 64, 128), jnp.float32)
        _lenS = 64 - jax.random.randint(jax.random.fold_in(_rk, 7), (32,), 0, max(1, 64 // 4) + 1, jnp.int32)
        _lenS2 = 64 - jax.random.randint(jax.random.fold_in(_rk, 8), (32,), 0, max(1, 64 // 4) + 1, jnp.int32)
        _ctx_1024P = jax.random.normal(jax.random.fold_in(_rk, 11), (32, 16, 128), jnp.float32)
        _ctx_1024c = jax.random.dirichlet(jax.random.fold_in(_rk, 511), 0.3 * jnp.ones((16,), jnp.float32), (32, 64))
        _ctx_1024t = jnp.einsum('bsk,bkd->bsd', _ctx_1024c, _ctx_1024P)
        _ctx_1024t = _ctx_1024t * jax.lax.rsqrt(jnp.mean(jnp.square(_ctx_1024t)) + 1e-12) * 0.953939
        ctx_1024 = 2.81802e-05 + 1.00001 * (_ctx_1024t + 0.3 * jax.random.normal(jax.random.fold_in(_rk, 611), (32, 64, 128), jnp.float32))
        _validS = jnp.arange(64)[None, :] < _lenS[:, None]
        _validS2 = jnp.arange(64)[None, :] < _lenS2[:, None]
        _causal = jnp.tril(jnp.ones((64, 64), dtype=bool))
        mask_BxS2_ik0 = jnp.where(jnp.broadcast_to(_validS2[:, :], (32, 64)), 0, 1).astype(jnp.int32)
        return (x, ctx_1024, mask_BxS2_ik0)
    x, ctx_1024, mask_BxS2_ik0 = _rec_inputs()

    def _L0_attn_setup():
        import jax, jax.numpy as jnp
        import numpy as np
        DIM = 128
        N_HEADS = 16
        HEAD_DIM = DIM // N_HEADS

        def apply_rope(x):
            B, T, H, D = x.shape
            half = D // 2
            x1, x2 = (x[..., :half], x[..., half:])
            theta = 1.0 / 10000.0 ** (jnp.arange(0, half, 2, dtype=jnp.float32) / half)
            pos = jnp.arange(T, dtype=jnp.float32)
            freq = pos[:, None] * theta[None, :]
            sin = jnp.sin(freq)[None, :, None, :]
            cos = jnp.cos(freq)[None, :, None, :]
            x1e, x1o = (x1[..., ::2], x1[..., 1::2])
            x2e, x2o = (x2[..., ::2], x2[..., 1::2])
            x1r = jnp.concatenate([x1e * cos - x1o * sin, x1e * sin + x1o * cos], axis=-1)
            x2r = jnp.concatenate([x2e * cos - x2o * sin, x2e * sin + x2o * cos], axis=-1)
            return jnp.concatenate([x1r, x2r], axis=-1)
        key = jax.random.key(seed)
        ks = jax.random.split(key, 9)
        B, T, C, D = (2, 256, DIM, HEAD_DIM)
        s = 0.02
        return {'x': jax.random.normal(ks[0], (B, T, C), dtype=jnp.float32), 'Wq': jax.random.normal(ks[1], (C, C), dtype=jnp.float32) * s, 'bq': jnp.zeros((C,), dtype=jnp.float32), 'Wk': jax.random.normal(ks[2], (C, D), dtype=jnp.float32) * s, 'bk': jnp.zeros((D,), dtype=jnp.float32), 'Wv': jax.random.normal(ks[3], (C, D), dtype=jnp.float32) * s, 'bv': jnp.zeros((D,), dtype=jnp.float32), 'Wo': jax.random.normal(ks[4], (C, C), dtype=jnp.float32) * s, 'bo': jnp.zeros((C,), dtype=jnp.float32)}
    _L0_attn_all = _L0_attn_setup()
    _L0_attn_in = {k: v for k, v in _L0_attn_all.items() if k in ('Wq', 'bq', 'Wk', 'bk', 'Wv', 'bv', 'Wo', 'bo')}
    del _L0_attn_all

    def _L0_xattn_setup():
        import jax, jax.numpy as jnp
        import numpy as np
        ALPHA = 1.5
        EPS = 1e-10

        def quat_mul(a, b):
            aw, ax, ay, az = jnp.split(a, 4, axis=-1)
            bw, bx, by, bz = jnp.split(b, 4, axis=-1)
            w = aw * bw - ax * bx - ay * by - az * bz
            x = aw * bx + ax * bw + ay * bz - az * by
            y = aw * by - ax * bz + ay * bw + az * bx
            z = aw * bz + ax * by - ay * bx + az * bw
            return jnp.concatenate([w, x, y, z], axis=-1)
        key = jax.random.key(seed)
        ks = jax.random.split(key, 8)
        B, S, D = (8, 256, 128)
        scale = 1.0 / np.sqrt(D)
        return {'query': jax.random.normal(ks[0], (B, S, D), dtype=jnp.float32), 'memory': jax.random.normal(ks[1], (B, S, D), dtype=jnp.float32), 'wq': jax.random.normal(ks[2], (D, D), dtype=jnp.float32) * scale, 'bq': jax.random.normal(ks[3], (D,), dtype=jnp.float32) * scale, 'wk': jax.random.normal(ks[4], (D, D), dtype=jnp.float32) * scale, 'bk': jax.random.normal(ks[5], (D,), dtype=jnp.float32) * scale, 'wv': jax.random.normal(ks[6], (D, D), dtype=jnp.float32) * scale, 'bv': jax.random.normal(ks[7], (D,), dtype=jnp.float32) * scale}
    _L0_xattn_all = _L0_xattn_setup()
    _L0_xattn_in = {k: v for k, v in _L0_xattn_all.items() if k in ('wq', 'bq', 'wk', 'bk', 'wv', 'bv')}
    del _L0_xattn_all

    def _L0_ffn_setup():
        import jax, jax.numpy as jnp
        import numpy as np
        DIM = 128
        MLP_MULT = 4
        NUM_EXPERTS = 8
        EXPERT_HIDDEN = MLP_MULT * DIM // NUM_EXPERTS
        key = jax.random.key(seed)
        k_x, k_r, k_fc, k_pj = jax.random.split(key, 4)
        x = jax.random.normal(k_x, (4, 512, DIM), dtype=jnp.float32)
        w_router = jax.random.normal(k_r, (NUM_EXPERTS, DIM), dtype=jnp.float32) * (1.0 / np.sqrt(DIM))
        w_fc = jax.random.normal(k_fc, (NUM_EXPERTS, EXPERT_HIDDEN, DIM), dtype=jnp.float32) * (1.0 / np.sqrt(DIM))
        w_proj = jax.random.normal(k_pj, (NUM_EXPERTS, DIM, EXPERT_HIDDEN), dtype=jnp.float32) * (1.0 / np.sqrt(EXPERT_HIDDEN))
        return {'x': x, 'w_router': w_router, 'w_fc': w_fc, 'w_proj': w_proj}
    _L0_ffn_all = _L0_ffn_setup()
    _L0_ffn_in = {k: v for k, v in _L0_ffn_all.items() if k in ('w_router', 'w_fc', 'w_proj')}
    del _L0_ffn_all

    def _L1_attn_setup():
        import jax, jax.numpy as jnp
        import numpy as np

        def log_g(x):
            pos = jnp.log(jnp.maximum(x, 0.0) + 0.5)
            neg = -jax.nn.softplus(-x)
            return jnp.where(x >= 0, pos, neg)

        def parallel_scan_log(log_coeffs, log_values):
            a_star = jnp.cumsum(log_coeffs, axis=1)
            log_h0_plus_b_star = jax.lax.cumlogsumexp(log_values - a_star, axis=1)
            log_h = a_star + log_h0_plus_b_star
            return jnp.exp(log_h)
        key = jax.random.key(seed)
        k1, k2 = jax.random.split(key)
        B, S, D = (8, 512, 128)
        x = jax.random.normal(k1, (B, S, D), dtype=jnp.float32)
        W_hg = jax.random.normal(k2, (2 * D, D), dtype=jnp.float32) * (1.0 / np.sqrt(D))
        return {'x': x, 'W_hg': W_hg}
    _L1_attn_all = _L1_attn_setup()
    _L1_attn_in = {k: v for k, v in _L1_attn_all.items() if k in ('W_hg',)}
    del _L1_attn_all

    def _L1_xattn_setup():
        import jax, jax.numpy as jnp
        import numpy as np
        B, LQ, LK, D = (4, 256, 256, 128)
        H = 16
        HD = D // H

        def _split_heads(x):
            b, l, _ = x.shape
            return x.reshape(b, l, H, HD).transpose(0, 2, 1, 3)
        key = jax.random.key(seed)
        ks = jax.random.split(key, 10)
        s = 0.02
        return {'hidden_states': jax.random.normal(ks[0], (B, LQ, D), jnp.float32), 'context': jax.random.normal(ks[1], (B, LK, D), jnp.float32), 'attention_mask': jax.random.randint(ks[2], (B, LK), 0, 2, jnp.int32), 'q_w': jax.random.normal(ks[3], (D, D), jnp.float32) * s, 'q_b': jnp.zeros((D,), jnp.float32), 'k_w': jax.random.normal(ks[4], (D, D), jnp.float32) * s, 'k_b': jnp.zeros((D,), jnp.float32), 'v_w': jax.random.normal(ks[5], (D, D), jnp.float32) * s, 'v_b': jnp.zeros((D,), jnp.float32)}
    _L1_xattn_all = _L1_xattn_setup()
    _L1_xattn_in = {k: v for k, v in _L1_xattn_all.items() if k in ('q_w', 'q_b', 'k_w', 'k_b', 'v_w', 'v_b')}
    del _L1_xattn_all

    def _L1_ffn_setup():
        import jax, jax.numpy as jnp
        import numpy as np
        B, S, D_MODEL, D_HIDDEN = (4, 256, 128, 512)

        def act_quant(x):
            scale = 127.0 / jnp.clip(jnp.max(jnp.abs(x), axis=-1, keepdims=True), 1e-05)
            return jnp.clip(jnp.round(x * scale), -128, 127) / scale

        def weight_quant(w):
            scale = 1.0 / jnp.clip(jnp.mean(jnp.abs(w)), 1e-05)
            return jnp.clip(jnp.round(w * scale), -1, 1) / scale

        def bit_linear(x, w):
            xq = x + jax.lax.stop_gradient(act_quant(x) - x)
            wq = w + jax.lax.stop_gradient(weight_quant(w) - w)
            return jnp.einsum('bsd,hd->bsh', xq, wq)

        def depthwise_conv1d(x_bcl, w, b):
            y = jax.lax.conv_general_dilated(x_bcl, w, window_strides=(1,), padding=[(1, 1)], dimension_numbers=('NCH', 'OIH', 'NCH'), feature_group_count=x_bcl.shape[1])
            return y + b[None, :, None]
        key = jax.random.key(seed)
        ks = jax.random.split(key, 5)
        lim1 = 1.0 / np.sqrt(D_MODEL)
        lim2 = 1.0 / np.sqrt(D_HIDDEN)
        limc = 1.0 / np.sqrt(3.0)
        return {'x': jax.random.normal(ks[0], (B, S, D_MODEL), dtype=jnp.float32), 'w1': jax.random.uniform(ks[1], (D_HIDDEN, D_MODEL), jnp.float32, -lim1, lim1), 'conv_w': jax.random.uniform(ks[2], (D_HIDDEN, 1, 3), jnp.float32, -limc, limc), 'conv_b': jax.random.uniform(ks[3], (D_HIDDEN,), jnp.float32, -limc, limc), 'w2': jax.random.uniform(ks[4], (D_MODEL, D_HIDDEN), jnp.float32, -lim2, lim2)}
    _L1_ffn_all = _L1_ffn_setup()
    _L1_ffn_in = {k: v for k, v in _L1_ffn_all.items() if k in ('w1', 'conv_w', 'conv_b', 'w2')}
    del _L1_ffn_all

    def _L2_attn_setup():
        import jax, jax.numpy as jnp
        import numpy as np
        from jax import lax
        NEG_INF = -1e+38

        def wkv(time_decay, u, k, v):
            w = -jnp.exp(time_decay)
            B, T, C = k.shape

            def step(carry, kv):
                aa, bb, pp = carry
                kt, vt = kv
                ww = u + kt
                p = jnp.maximum(pp, ww)
                e1 = jnp.exp(pp - p)
                e2 = jnp.exp(ww - p)
                y = (e1 * aa + e2 * vt) / (e1 * bb + e2)
                ww2 = pp + w
                p2 = jnp.maximum(ww2, kt)
                e1b = jnp.exp(ww2 - p2)
                e2b = jnp.exp(kt - p2)
                return ((e1b * aa + e2b * vt, e1b * bb + e2b, p2), y)
            init = (jnp.zeros((B, C), k.dtype), jnp.zeros((B, C), k.dtype), jnp.full((B, C), NEG_INF, k.dtype))
            ks = jnp.moveaxis(k, 1, 0)
            vs = jnp.moveaxis(v, 1, 0)
            _, ys = lax.scan(step, init, (ks, vs))
            return jnp.moveaxis(ys, 0, 1)
        key = jax.random.key(seed)
        ks = jax.random.split(key, 10)
        B, T, C = (32, 128, 128)
        return {'x': jax.random.normal(ks[0], (B, T, C), jnp.float32), 'time_decay': jax.random.normal(ks[1], (C,), jnp.float32) * 0.5, 'time_first': jax.random.normal(ks[2], (C,), jnp.float32) * 0.5 + np.log(0.3).astype(np.float32), 'time_mix_k': jax.random.uniform(ks[3], (1, 1, C), jnp.float32), 'time_mix_v': jax.random.uniform(ks[4], (1, 1, C), jnp.float32), 'time_mix_r': jax.random.uniform(ks[5], (1, 1, C), jnp.float32), 'Wk': jax.random.normal(ks[6], (C, C), jnp.float32) * 0.02, 'Wv': jax.random.normal(ks[7], (C, C), jnp.float32) * 0.02, 'Wr': jax.random.normal(ks[8], (C, C), jnp.float32) * 0.02, 'Wo': jax.random.normal(ks[9], (C, C), jnp.float32) * 0.02}
    _L2_attn_all = _L2_attn_setup()
    _L2_attn_in = {k: v for k, v in _L2_attn_all.items() if k in ('time_decay', 'time_first', 'time_mix_k', 'time_mix_v', 'time_mix_r', 'Wk', 'Wv', 'Wr', 'Wo')}
    del _L2_attn_all

    def _L2_xattn_setup():
        import jax, jax.numpy as jnp
        import numpy as np
        EMBED_DIM = 128
        NUM_HEADS = 16
        HEAD_DIM = EMBED_DIM // NUM_HEADS
        key = jax.random.key(seed)
        ks = jax.random.split(key, 7)
        B, S, E = (2, 256, EMBED_DIM)
        bound = float(np.sqrt(6.0 / (E + E)))
        mkw = lambda k: jax.random.uniform(k, (E, E), jnp.float32, -bound, bound)
        return {'query': jax.random.normal(ks[0], (B, S, E), jnp.float32), 'key': jax.random.normal(ks[1], (B, S, E), jnp.float32), 'value': jax.random.normal(ks[2], (B, S, E), jnp.float32), 'Wq': mkw(ks[3]), 'Wk': mkw(ks[4]), 'Wv': mkw(ks[5]), 'Wo': mkw(ks[6])}
    _L2_xattn_all = _L2_xattn_setup()
    _L2_xattn_in = {k: v for k, v in _L2_xattn_all.items() if k in ('Wq', 'Wk', 'Wv', 'Wo')}
    del _L2_xattn_all

    def _L2_ffn_setup():
        import jax, jax.numpy as jnp
        import numpy as np
        BLOCK = 16
        _GRID = jnp.array([0.0, 0.5, 1.0, 1.5, 2.0, 3.0, 4.0, 6.0], dtype=jnp.float32)
        _MID = jnp.array([0.25, 0.75, 1.25, 1.75, 2.5, 3.5, 5.0], dtype=jnp.float32)

        def fp4_quant_dequant(x):
            shape = x.shape
            xb = x.reshape(shape[:-1] + (shape[-1] // BLOCK, BLOCK))
            scale = jnp.max(jnp.abs(xb), axis=-1, keepdims=True) / 6.0
            scale = jnp.maximum(scale, jnp.float32(1e-12))
            xn = xb / scale
            idx = jnp.searchsorted(_MID, jnp.abs(xn))
            q = _GRID[idx] * jnp.sign(xn) * scale
            return q.reshape(shape)

        def fp4_linear(x, w):
            xq = fp4_quant_dequant(x)
            wq = fp4_quant_dequant(w)
            return jnp.einsum('bsk,nk->bsn', xq, wq)
        key = jax.random.key(seed)
        k1, k2, k3, k4 = jax.random.split(key, 4)
        H, I = (128, 352)
        x = jax.random.normal(k1, (4, 512, H), dtype=jnp.float32)
        w_gate = jax.random.normal(k2, (I, H), dtype=jnp.float32) * 0.02
        w_up = jax.random.normal(k3, (I, H), dtype=jnp.float32) * 0.02
        w_down = jax.random.normal(k4, (H, I), dtype=jnp.float32) * 0.02
        return {'x': x, 'w_gate': w_gate, 'w_up': w_up, 'w_down': w_down}
    _L2_ffn_all = _L2_ffn_setup()
    _L2_ffn_in = {k: v for k, v in _L2_ffn_all.items() if k in ('w_gate', 'w_up', 'w_down')}
    del _L2_ffn_all

    def _L3_attn_setup():
        import jax, jax.numpy as jnp
        import numpy as np
        B, S, D = (4, 256, 128)
        H = 16
        HS = D // H
        SCALE = HS ** 0.5
        key = jax.random.key(seed)
        ks = jax.random.split(key, 9)
        std = 1.0 / np.sqrt(D)

        def lin(kw, kb, fan_in, fan_out):
            w = jax.random.uniform(kw, (fan_in, fan_out), minval=-std, maxval=std, dtype=jnp.float32)
            b = jax.random.uniform(kb, (fan_out,), minval=-std, maxval=std, dtype=jnp.float32)
            return (w, b)
        Wq, bq = lin(ks[0], ks[1], D, D)
        Wk, bk = lin(ks[2], ks[3], D, D)
        Wv, bv = lin(ks[4], ks[5], D, D)
        Wm, bm = lin(ks[6], ks[7], D, D)
        x = jax.random.normal(ks[8], (B, S, D), dtype=jnp.float32)
        return {'x': x, 'Wq': Wq, 'bq': bq, 'Wk': Wk, 'bk': bk, 'Wv': Wv, 'bv': bv, 'Wm': Wm, 'bm': bm}
    _L3_attn_all = _L3_attn_setup()
    _L3_attn_in = {k: v for k, v in _L3_attn_all.items() if k in ('Wq', 'bq', 'Wk', 'bk', 'Wv', 'bv', 'Wm', 'bm')}
    del _L3_attn_all

    def _L3_xattn_setup():
        import jax, jax.numpy as jnp
        import numpy as np
        BETA = 128
        NUM_HEADS = 16
        NORM = (BETA // NUM_HEADS) ** (-0.5)
        key = jax.random.key(seed)
        ks = jax.random.split(key, 6)
        B, N = (4, 256)
        D_in_q = D_in_k = D_in_v = 128
        D_out_k = D_out_v = 128
        q = jax.random.normal(ks[0], (B, N, D_in_q), dtype=jnp.float32)
        k = jax.random.normal(ks[1], (B, N, D_in_k), dtype=jnp.float32)
        v = jax.random.normal(ks[2], (B, N, D_in_v), dtype=jnp.float32)
        Wq = jax.random.normal(ks[3], (D_out_k, D_in_q), dtype=jnp.float32) * D_in_q ** (-0.5)
        Wk = jax.random.normal(ks[4], (D_out_k, D_in_k), dtype=jnp.float32) * D_in_k ** (-0.5)
        Wv = jax.random.normal(ks[5], (D_out_v, D_in_v), dtype=jnp.float32) * D_in_v ** (-0.5)
        return {'q': q, 'k': k, 'v': v, 'Wq': Wq, 'Wk': Wk, 'Wv': Wv}
    _L3_xattn_all = _L3_xattn_setup()
    _L3_xattn_in = {k: v for k, v in _L3_xattn_all.items() if k in ('Wq', 'Wk', 'Wv')}
    del _L3_xattn_all

    def _L3_ffn_setup():
        import jax, jax.numpy as jnp
        import numpy as np
        B, S, D, FF, E, L = (8, 256, 128, 512, 16, 4)

        def _unipool_layer(xt, router, W1, W2):
            logits = xt @ router
            probs = jax.nn.softmax(logits, axis=-1)
            w = jnp.max(probs, axis=-1)
            idx = jnp.argmax(probs, axis=-1)

            def body(acc, params):
                w1, w2, i = params
                h = jax.nn.silu(xt @ w1) @ w2
                sel = jnp.where(idx == i, w, 0.0)
                return (acc + sel[:, None] * h, None)
            out, _ = jax.lax.scan(body, jnp.zeros_like(xt), (W1, W2, jnp.arange(W1.shape[0])))
            return out
        key = jax.random.key(seed)
        k0, k1, k2, k3 = jax.random.split(key, 4)
        x = jax.random.normal(k0, (B, S, D), dtype=jnp.float32)
        routers = jax.random.normal(k1, (L, D, E), dtype=jnp.float32) * 0.02
        W1 = jax.random.normal(k2, (E, D, FF), dtype=jnp.float32) * 0.02
        W2 = jax.random.normal(k3, (E, FF, D), dtype=jnp.float32) * 0.02
        return {'x': x, 'routers': routers, 'W1': W1, 'W2': W2}
    _L3_ffn_all = _L3_ffn_setup()
    _L3_ffn_in = {k: v for k, v in _L3_ffn_all.items() if k in ('routers', 'W1', 'W2')}
    del _L3_ffn_all
    return {'x': x, 'ctx_1024': ctx_1024, 'mask_BxS2_ik0': mask_BxS2_ik0, 'L0_attn_Wq': _L0_attn_in['Wq'], 'L0_attn_bq': _L0_attn_in['bq'], 'L0_attn_Wk': _L0_attn_in['Wk'], 'L0_attn_bk': _L0_attn_in['bk'], 'L0_attn_Wv': _L0_attn_in['Wv'], 'L0_attn_bv': _L0_attn_in['bv'], 'L0_attn_Wo': _L0_attn_in['Wo'], 'L0_attn_bo': _L0_attn_in['bo'], 'L0_xattn_wq': _L0_xattn_in['wq'], 'L0_xattn_bq': _L0_xattn_in['bq'], 'L0_xattn_wk': _L0_xattn_in['wk'], 'L0_xattn_bk': _L0_xattn_in['bk'], 'L0_xattn_wv': _L0_xattn_in['wv'], 'L0_xattn_bv': _L0_xattn_in['bv'], 'L0_ffn_w_router': _L0_ffn_in['w_router'], 'L0_ffn_w_fc': _L0_ffn_in['w_fc'], 'L0_ffn_w_proj': _L0_ffn_in['w_proj'], 'L1_attn_W_hg': _L1_attn_in['W_hg'], 'L1_xattn_q_w': _L1_xattn_in['q_w'], 'L1_xattn_q_b': _L1_xattn_in['q_b'], 'L1_xattn_k_w': _L1_xattn_in['k_w'], 'L1_xattn_k_b': _L1_xattn_in['k_b'], 'L1_xattn_v_w': _L1_xattn_in['v_w'], 'L1_xattn_v_b': _L1_xattn_in['v_b'], 'L1_ffn_w1': _L1_ffn_in['w1'], 'L1_ffn_conv_w': _L1_ffn_in['conv_w'], 'L1_ffn_conv_b': _L1_ffn_in['conv_b'], 'L1_ffn_w2': _L1_ffn_in['w2'], 'L2_attn_time_decay': _L2_attn_in['time_decay'], 'L2_attn_time_first': _L2_attn_in['time_first'], 'L2_attn_time_mix_k': _L2_attn_in['time_mix_k'], 'L2_attn_time_mix_v': _L2_attn_in['time_mix_v'], 'L2_attn_time_mix_r': _L2_attn_in['time_mix_r'], 'L2_attn_Wk': _L2_attn_in['Wk'], 'L2_attn_Wv': _L2_attn_in['Wv'], 'L2_attn_Wr': _L2_attn_in['Wr'], 'L2_attn_Wo': _L2_attn_in['Wo'], 'L2_xattn_Wq': _L2_xattn_in['Wq'], 'L2_xattn_Wk': _L2_xattn_in['Wk'], 'L2_xattn_Wv': _L2_xattn_in['Wv'], 'L2_xattn_Wo': _L2_xattn_in['Wo'], 'L2_ffn_w_gate': _L2_ffn_in['w_gate'], 'L2_ffn_w_up': _L2_ffn_in['w_up'], 'L2_ffn_w_down': _L2_ffn_in['w_down'], 'L3_attn_Wq': _L3_attn_in['Wq'], 'L3_attn_bq': _L3_attn_in['bq'], 'L3_attn_Wk': _L3_attn_in['Wk'], 'L3_attn_bk': _L3_attn_in['bk'], 'L3_attn_Wv': _L3_attn_in['Wv'], 'L3_attn_bv': _L3_attn_in['bv'], 'L3_attn_Wm': _L3_attn_in['Wm'], 'L3_attn_bm': _L3_attn_in['bm'], 'L3_xattn_Wq': _L3_xattn_in['Wq'], 'L3_xattn_Wk': _L3_xattn_in['Wk'], 'L3_xattn_Wv': _L3_xattn_in['Wv'], 'L3_ffn_routers': _L3_ffn_in['routers'], 'L3_ffn_W1': _L3_ffn_in['W1'], 'L3_ffn_W2': _L3_ffn_in['W2']}

def reference(x, ctx_1024, mask_BxS2_ik0, L0_attn_Wq, L0_attn_bq, L0_attn_Wk, L0_attn_bk, L0_attn_Wv, L0_attn_bv, L0_attn_Wo, L0_attn_bo, L0_xattn_wq, L0_xattn_bq, L0_xattn_wk, L0_xattn_bk, L0_xattn_wv, L0_xattn_bv, L0_ffn_w_router, L0_ffn_w_fc, L0_ffn_w_proj, L1_attn_W_hg, L1_xattn_q_w, L1_xattn_q_b, L1_xattn_k_w, L1_xattn_k_b, L1_xattn_v_w, L1_xattn_v_b, L1_ffn_w1, L1_ffn_conv_w, L1_ffn_conv_b, L1_ffn_w2, L2_attn_time_decay, L2_attn_time_first, L2_attn_time_mix_k, L2_attn_time_mix_v, L2_attn_time_mix_r, L2_attn_Wk, L2_attn_Wv, L2_attn_Wr, L2_attn_Wo, L2_xattn_Wq, L2_xattn_Wk, L2_xattn_Wv, L2_xattn_Wo, L2_ffn_w_gate, L2_ffn_w_up, L2_ffn_w_down, L3_attn_Wq, L3_attn_bq, L3_attn_Wk, L3_attn_bk, L3_attn_Wv, L3_attn_bv, L3_attn_Wm, L3_attn_bm, L3_xattn_Wq, L3_xattn_Wk, L3_xattn_Wv, L3_ffn_routers, L3_ffn_W1, L3_ffn_W2):
    import jax
    import jax.numpy as jnp

    def _L0_attn_ref(x, Wq, bq, Wk, bk, Wv, bv, Wo, bo):
        import jax, jax.numpy as jnp
        import numpy as np
        DIM = 128
        N_HEADS = 16
        HEAD_DIM = DIM // N_HEADS

        def apply_rope(x):
            B, T, H, D = x.shape
            half = D // 2
            x1, x2 = (x[..., :half], x[..., half:])
            theta = 1.0 / 10000.0 ** (jnp.arange(0, half, 2, dtype=jnp.float32) / half)
            pos = jnp.arange(T, dtype=jnp.float32)
            freq = pos[:, None] * theta[None, :]
            sin = jnp.sin(freq)[None, :, None, :]
            cos = jnp.cos(freq)[None, :, None, :]
            x1e, x1o = (x1[..., ::2], x1[..., 1::2])
            x2e, x2o = (x2[..., ::2], x2[..., 1::2])
            x1r = jnp.concatenate([x1e * cos - x1o * sin, x1e * sin + x1o * cos], axis=-1)
            x2r = jnp.concatenate([x2e * cos - x2o * sin, x2e * sin + x2o * cos], axis=-1)
            return jnp.concatenate([x1r, x2r], axis=-1)
        B, T, C = x.shape
        H, D = (N_HEADS, HEAD_DIM)
        q = (x @ Wq + bq).reshape(B, T, H, D).transpose(0, 2, 1, 3)
        k = x @ Wk + bk
        v = x @ Wv + bv
        q = apply_rope(q)
        k = apply_rope(k[:, None])[:, 0]
        scores = jnp.einsum('bhtd,bsd->bhts', q, k) / jnp.sqrt(jnp.float32(D))
        mask = jnp.tril(jnp.ones((T, T), dtype=bool))
        scores = jnp.where(mask[None, None], scores, -jnp.inf)
        probs = jax.nn.softmax(scores, axis=-1)
        attn = jnp.einsum('bhts,bsd->bhtd', probs, v)
        attn = attn.transpose(0, 2, 1, 3).reshape(B, T, C)
        return attn @ Wo + bo

    def _L0_xattn_ref(query, memory, wq, bq, wk, bk, wv, bv):
        import jax, jax.numpy as jnp
        import numpy as np
        ALPHA = 1.5
        EPS = 1e-10

        def quat_mul(a, b):
            aw, ax, ay, az = jnp.split(a, 4, axis=-1)
            bw, bx, by, bz = jnp.split(b, 4, axis=-1)
            w = aw * bw - ax * bx - ay * by - az * bz
            x = aw * bx + ax * bw + ay * bz - az * by
            y = aw * by - ax * bz + ay * bw + az * bx
            z = aw * bz + ax * by - ay * bx + az * bw
            return jnp.concatenate([w, x, y, z], axis=-1)
        Q = query @ wq + bq
        K = memory @ wk + bk
        V = memory @ wv + bv
        Qf = jnp.fft.fft(Q, axis=-2)
        Kf = jnp.fft.fft(K, axis=-2)
        Vf = jnp.fft.fft(V, axis=-2)
        S = Q.shape[-2]
        k = jnp.arange(S, dtype=jnp.float32)
        filt = jnp.exp(1j * ALPHA * jnp.arctan(jnp.log(k + EPS)))[:, None]
        Qf = Qf * filt
        Kf = Kf * filt
        Vf = Vf * filt
        qkv = quat_mul(quat_mul(Qf, Kf), Vf)
        attended = jnp.fft.ifft(qkv, axis=-2).real
        return attended

    def _L0_ffn_ref(x, w_router, w_fc, w_proj):
        import jax, jax.numpy as jnp
        import numpy as np
        DIM = 128
        MLP_MULT = 4
        NUM_EXPERTS = 8
        EXPERT_HIDDEN = MLP_MULT * DIM // NUM_EXPERTS
        logits = jnp.einsum('bsd,ed->bse', jax.lax.stop_gradient(x), w_router)
        weights = jax.nn.softmax(logits, axis=-1)
        indices = jnp.argmax(weights, axis=-1)
        onehot = jax.nn.one_hot(indices, NUM_EXPERTS, dtype=x.dtype)
        h = jnp.einsum('bsd,ehd->bseh', x, w_fc)
        h = jnp.where(h >= 0, h, 0.5 * h)
        h = h * h
        out = jnp.einsum('bseh,edh,bse->bsd', h, w_proj, onehot)
        return out

    def _L1_attn_ref(x, W_hg):
        import jax, jax.numpy as jnp
        import numpy as np

        def log_g(x):
            pos = jnp.log(jnp.maximum(x, 0.0) + 0.5)
            neg = -jax.nn.softplus(-x)
            return jnp.where(x >= 0, pos, neg)

        def parallel_scan_log(log_coeffs, log_values):
            a_star = jnp.cumsum(log_coeffs, axis=1)
            log_h0_plus_b_star = jax.lax.cumlogsumexp(log_values - a_star, axis=1)
            log_h = a_star + log_h0_plus_b_star
            return jnp.exp(log_h)
        hg = jnp.einsum('bsd,ed->bse', x, W_hg)
        hidden, gate = jnp.split(hg, 2, axis=-1)
        log_coeffs = -jax.nn.softplus(gate)
        log_z = -jax.nn.softplus(-gate)
        log_tilde_h = log_g(hidden)
        log_values = log_z + log_tilde_h
        out = parallel_scan_log(log_coeffs, log_values)
        return out

    def _L1_xattn_ref(hidden_states, context, attention_mask, q_w, q_b, k_w, k_b, v_w, v_b):
        import jax, jax.numpy as jnp
        import numpy as np
        B, LQ, LK, D = (4, 256, 256, 128)
        H = 16
        HD = D // H

        def _split_heads(x):
            b, l, _ = x.shape
            return x.reshape(b, l, H, HD).transpose(0, 2, 1, 3)
        q = _split_heads(hidden_states @ q_w.T + q_b)
        k = _split_heads(context @ k_w.T + k_b)
        v = _split_heads(context @ v_w.T + v_b)
        scores = jnp.einsum('bhqd,bhkd->bhqk', q, k) / jnp.sqrt(jnp.float32(HD))
        mask = (attention_mask > 0)[:, None, None, :]
        scores = jnp.where(mask, -jnp.inf, scores)
        probs = jax.nn.softmax(scores, axis=-1)
        ctx = jnp.einsum('bhqk,bhkd->bhqd', probs, v)
        ctx = ctx.transpose(0, 2, 1, 3).reshape(ctx.shape[0], ctx.shape[2], H * HD)
        return ctx

    def _L1_ffn_ref(x, w1, conv_w, conv_b, w2):
        import jax, jax.numpy as jnp
        import numpy as np
        B, S, D_MODEL, D_HIDDEN = (4, 256, 128, 512)

        def act_quant(x):
            scale = 127.0 / jnp.clip(jnp.max(jnp.abs(x), axis=-1, keepdims=True), 1e-05)
            return jnp.clip(jnp.round(x * scale), -128, 127) / scale

        def weight_quant(w):
            scale = 1.0 / jnp.clip(jnp.mean(jnp.abs(w)), 1e-05)
            return jnp.clip(jnp.round(w * scale), -1, 1) / scale

        def bit_linear(x, w):
            xq = x + jax.lax.stop_gradient(act_quant(x) - x)
            wq = w + jax.lax.stop_gradient(weight_quant(w) - w)
            return jnp.einsum('bsd,hd->bsh', xq, wq)

        def depthwise_conv1d(x_bcl, w, b):
            y = jax.lax.conv_general_dilated(x_bcl, w, window_strides=(1,), padding=[(1, 1)], dimension_numbers=('NCH', 'OIH', 'NCH'), feature_group_count=x_bcl.shape[1])
            return y + b[None, :, None]
        h = bit_linear(x, w1)
        h = depthwise_conv1d(h.transpose(0, 2, 1), conv_w, conv_b)
        h = h.transpose(0, 2, 1)
        h = jax.nn.silu(h)
        return bit_linear(h, w2)

    def _L2_attn_ref(x, time_decay, time_first, time_mix_k, time_mix_v, time_mix_r, Wk, Wv, Wr, Wo):
        import jax, jax.numpy as jnp
        import numpy as np
        from jax import lax
        NEG_INF = -1e+38

        def wkv(time_decay, u, k, v):
            w = -jnp.exp(time_decay)
            B, T, C = k.shape

            def step(carry, kv):
                aa, bb, pp = carry
                kt, vt = kv
                ww = u + kt
                p = jnp.maximum(pp, ww)
                e1 = jnp.exp(pp - p)
                e2 = jnp.exp(ww - p)
                y = (e1 * aa + e2 * vt) / (e1 * bb + e2)
                ww2 = pp + w
                p2 = jnp.maximum(ww2, kt)
                e1b = jnp.exp(ww2 - p2)
                e2b = jnp.exp(kt - p2)
                return ((e1b * aa + e2b * vt, e1b * bb + e2b, p2), y)
            init = (jnp.zeros((B, C), k.dtype), jnp.zeros((B, C), k.dtype), jnp.full((B, C), NEG_INF, k.dtype))
            ks = jnp.moveaxis(k, 1, 0)
            vs = jnp.moveaxis(v, 1, 0)
            _, ys = lax.scan(step, init, (ks, vs))
            return jnp.moveaxis(ys, 0, 1)
        xx = jnp.pad(x, ((0, 0), (1, 0), (0, 0)))[:, :-1]
        xk = x * time_mix_k + xx * (1.0 - time_mix_k)
        xv = x * time_mix_v + xx * (1.0 - time_mix_v)
        xr = x * time_mix_r + xx * (1.0 - time_mix_r)
        k = jnp.einsum('btc,oc->bto', xk, Wk)
        v = jnp.einsum('btc,oc->bto', xv, Wv)
        r = jnp.einsum('btc,oc->bto', xr, Wr)
        rwkv = jax.nn.sigmoid(r) * wkv(time_decay, time_first, k, v)
        return jnp.einsum('btc,oc->bto', rwkv, Wo)

    def _L2_xattn_ref(query, key, value, Wq, Wk, Wv, Wo):
        import jax, jax.numpy as jnp
        import numpy as np
        EMBED_DIM = 128
        NUM_HEADS = 16
        HEAD_DIM = EMBED_DIM // NUM_HEADS
        B, L, E = query.shape
        H, D = (NUM_HEADS, HEAD_DIM)
        scale = D ** (-0.5)
        q = (query @ Wq.T).reshape(B, L, H, D) * scale
        k = (key @ Wk.T).reshape(B, -1, H, D)
        v = (value @ Wv.T).reshape(B, -1, H, D)
        scores = jax.nn.sigmoid(jnp.einsum('blhd,bshd->bhls', q, k))
        o = jnp.einsum('bhls,bshd->blhd', scores, v).reshape(B, L, E)
        return o @ Wo.T

    def _L2_ffn_ref(x, w_gate, w_up, w_down):
        import jax, jax.numpy as jnp
        import numpy as np
        BLOCK = 16
        _GRID = jnp.array([0.0, 0.5, 1.0, 1.5, 2.0, 3.0, 4.0, 6.0], dtype=jnp.float32)
        _MID = jnp.array([0.25, 0.75, 1.25, 1.75, 2.5, 3.5, 5.0], dtype=jnp.float32)

        def fp4_quant_dequant(x):
            shape = x.shape
            xb = x.reshape(shape[:-1] + (shape[-1] // BLOCK, BLOCK))
            scale = jnp.max(jnp.abs(xb), axis=-1, keepdims=True) / 6.0
            scale = jnp.maximum(scale, jnp.float32(1e-12))
            xn = xb / scale
            idx = jnp.searchsorted(_MID, jnp.abs(xn))
            q = _GRID[idx] * jnp.sign(xn) * scale
            return q.reshape(shape)

        def fp4_linear(x, w):
            xq = fp4_quant_dequant(x)
            wq = fp4_quant_dequant(w)
            return jnp.einsum('bsk,nk->bsn', xq, wq)
        gate = fp4_linear(x, w_gate)
        y = fp4_linear(x, w_up)
        h = jax.nn.silu(gate) * y
        return fp4_linear(h, w_down)

    def _L3_attn_ref(x, Wq, bq, Wk, bk, Wv, bv, Wm, bm):
        import jax, jax.numpy as jnp
        import numpy as np
        B, S, D = (4, 256, 128)
        H = 16
        HS = D // H
        SCALE = HS ** 0.5
        bs, seq, _ = x.shape

        def heads(w, b):
            return (x @ w + b).reshape(bs, seq, H, HS).transpose(0, 2, 1, 3)
        q = heads(Wq, bq)
        k = heads(Wk, bk)
        v = heads(Wv, bv)
        scores = jnp.einsum('bhqd,bhkd->bhqk', q, k) / SCALE
        causal_mask = jnp.arange(seq)[None, :] > jnp.arange(seq)[:, None]
        scores = jnp.where(causal_mask, jnp.float32(-1000000000000.0), scores)
        probs = jax.nn.softmax(scores, axis=-1)
        attn = jnp.einsum('bhqk,bhkd->bhqd', probs, v)
        attn = attn.transpose(0, 2, 1, 3).reshape(bs, seq, H * HS)
        return attn @ Wm + bm

    def _L3_xattn_ref(q, k, v, Wq, Wk, Wv):
        import jax, jax.numpy as jnp
        import numpy as np
        BETA = 128
        NUM_HEADS = 16
        NORM = (BETA // NUM_HEADS) ** (-0.5)
        qp = jax.nn.relu(jnp.einsum('bnd,od->bno', q, Wq))
        kp = jax.nn.relu(jnp.einsum('bnd,od->bno', k, Wk))
        vp = jax.nn.relu(jnp.einsum('bnd,od->bno', v, Wv))
        B, N, D = qp.shape
        dh = D // NUM_HEADS
        qh = qp.reshape(B, N, NUM_HEADS, dh)
        kh = kp.reshape(B, N, NUM_HEADS, dh)
        vh = vp.reshape(B, N, NUM_HEADS, vp.shape[-1] // NUM_HEADS)
        E = NORM * jnp.einsum('bqhd,bkhd->bhqk', qh, kh)
        A = jax.nn.softmax(E, axis=-1)
        out = jnp.einsum('bhqk,bkhd->bqhd', A, vh)
        return out.reshape(B, N, -1)

    def _L3_ffn_ref(x, routers, W1, W2):
        import jax, jax.numpy as jnp
        import numpy as np
        B, S, D, FF, E, L = (8, 256, 128, 512, 16, 4)

        def _unipool_layer(xt, router, W1, W2):
            logits = xt @ router
            probs = jax.nn.softmax(logits, axis=-1)
            w = jnp.max(probs, axis=-1)
            idx = jnp.argmax(probs, axis=-1)

            def body(acc, params):
                w1, w2, i = params
                h = jax.nn.silu(xt @ w1) @ w2
                sel = jnp.where(idx == i, w, 0.0)
                return (acc + sel[:, None] * h, None)
            out, _ = jax.lax.scan(body, jnp.zeros_like(xt), (W1, W2, jnp.arange(W1.shape[0])))
            return out
        b, s, d = x.shape
        xt = x.reshape(-1, d)

        def step(carry, router):
            return (_unipool_layer(carry, router, W1, W2), None)
        xt, _ = jax.lax.scan(step, xt, routers)
        return xt.reshape(b, s, d)
    x = _layernorm(x + _L0_attn_ref(x, L0_attn_Wq, L0_attn_bq, L0_attn_Wk, L0_attn_bk, L0_attn_Wv, L0_attn_bv, L0_attn_Wo, L0_attn_bo), axis=-1)
    x = _layernorm(x + _L0_xattn_ref(x, ctx_1024, L0_xattn_wq, L0_xattn_bq, L0_xattn_wk, L0_xattn_bk, L0_xattn_wv, L0_xattn_bv), axis=-1)
    x = _layernorm(x + _L0_ffn_ref(x, L0_ffn_w_router, L0_ffn_w_fc, L0_ffn_w_proj), axis=-1)
    x = _layernorm(x + _L1_attn_ref(x, L1_attn_W_hg), axis=-1)
    x = _layernorm(x + _L1_xattn_ref(x, ctx_1024, mask_BxS2_ik0, L1_xattn_q_w, L1_xattn_q_b, L1_xattn_k_w, L1_xattn_k_b, L1_xattn_v_w, L1_xattn_v_b), axis=-1)
    x = _layernorm(x + _L1_ffn_ref(x, L1_ffn_w1, L1_ffn_conv_w, L1_ffn_conv_b, L1_ffn_w2), axis=-1)
    x = _layernorm(x + _L2_attn_ref(x, L2_attn_time_decay, L2_attn_time_first, L2_attn_time_mix_k, L2_attn_time_mix_v, L2_attn_time_mix_r, L2_attn_Wk, L2_attn_Wv, L2_attn_Wr, L2_attn_Wo), axis=-1)
    x = _layernorm(x + _L2_xattn_ref(x, ctx_1024, ctx_1024, L2_xattn_Wq, L2_xattn_Wk, L2_xattn_Wv, L2_xattn_Wo), axis=-1)
    x = _layernorm(x + _L2_ffn_ref(x, L2_ffn_w_gate, L2_ffn_w_up, L2_ffn_w_down), axis=-1)
    x = _layernorm(x + _L3_attn_ref(x, L3_attn_Wq, L3_attn_bq, L3_attn_Wk, L3_attn_bk, L3_attn_Wv, L3_attn_bv, L3_attn_Wm, L3_attn_bm), axis=-1)
    x = _layernorm(x + _L3_xattn_ref(x, ctx_1024, ctx_1024, L3_xattn_Wq, L3_xattn_Wk, L3_xattn_Wv), axis=-1)
    x = _layernorm(x + _L3_ffn_ref(x, L3_ffn_routers, L3_ffn_W1, L3_ffn_W2), axis=-1)
    return x

_drawn_inputs = setup_inputs


def setup_inputs(seed=0):
    import zlib

    import numpy as np

    out = dict(_drawn_inputs(seed))
    spreads = {'L0_attn_bq': (0.0, 0.8),
     'L0_attn_bk': (0.0, 2.0),
     'L0_attn_bv': (0.0, 0.1),
     'L0_attn_bo': (0.0, 0.1),
     'L1_xattn_q_b': (0.0, 0.8),
     'L1_xattn_k_b': (0.0, 2.0),
     'L1_xattn_v_b': (0.0, 0.381)}
    factors = {'L0_attn_Wq': 8.0,
     'L0_attn_Wk': 8.0,
     'L1_xattn_q_w': 8.0,
     'L1_xattn_k_w': 8.0,
     'L1_ffn_w1': 3.711,
     'L1_ffn_conv_w': 3.609,
     'L1_ffn_conv_b': 2.723,
     'L2_attn_time_decay': 8.0,
     'L2_attn_time_first': 8.0,
     'L2_attn_time_mix_k': 8.0,
     'L2_attn_time_mix_v': 8.0,
     'L2_attn_time_mix_r': 8.0,
     'L2_attn_Wk': 8.0,
     'L2_attn_Wv': 8.0,
     'L2_attn_Wr': 8.0,
     'L2_attn_Wo': 8.0,
     'L2_ffn_w_gate': 6.035,
     'L2_ffn_w_up': 5.88,
     'L2_ffn_w_down': 5.94,
     'L3_attn_Wq': 8.0,
     'L3_attn_bq': 33.387,
     'L3_attn_Wk': 8.0,
     'L3_attn_bk': 64.0}
    for name, (base, spread) in spreads.items():
        noise = np.random.default_rng([zlib.crc32(name.encode()), seed]).standard_normal(out[name].shape)
        drawn = base * np.exp(spread * noise) if base else spread * noise
        out[name] = jnp.asarray(drawn.astype(out[name].dtype))
    for name, factor in factors.items():
        out[name] = (out[name] * factor).astype(out[name].dtype)
    return out
```

```python
from contextlib import ExitStack

import numpy as np
import concourse.bass as bass
from concourse import mybir

F32 = mybir.dt.float32
BF16 = mybir.dt.bfloat16
I32 = mybir.dt.int32
U32 = mybir.dt.uint32
ALU = mybir.AluOpType
ACT = mybir.ActivationFunctionType
AX = mybir.AxisListType

BATCH, SEQ, D = 32, 64, 128
HEADS, HD = 16, 8
NTOK = BATCH * SEQ
TILES = 4
CHUNK = TILES * 128
CSEQ = CHUNK // SEQ
CHUNKS = 2
TOK = CHUNKS * CHUNK
PASSES = NTOK // TOK
EPS = 1e-5
NEG = -1e30
FIRST_PP = -1e38
ROUND = 12582912.0
FF8, NE8 = 64, 8
HID1 = 512
I2, BLK = 352, 16
NE, FF, ROUNDS = 16, 512, 4
HC = FF // 128


COLS = [
    ("ident", 128), ("ones", 128), ("head4", 4), ("cosr", 1), ("sinr", 1), ("causal", 64),
    ("dft_c", 128), ("dft_d", 128), ("dft_nd", 128), ("inv_c", 128), ("inv_ns", 128), ("sign", 256),
    ("desc8", 8), ("desc16", 16), ("spread8", 512), ("sel", 512),
    ("tri", 128), ("slots", 32), ("first", 256),
    ("a0q", 128), ("a0qs", 128), ("a0k", 128), ("a0v", 128), ("a0o", 128),
    ("a0bq", 1), ("a0bqs", 1), ("a0bk", 1),
    ("f_q", 256), ("f_k", 256), ("f_v", 256),
    ("m_r", 8), ("m_fc", 512), ("m_pj", 512),
    ("g_hg", 256),
    ("x1q", 128), ("x1k", 128), ("x1v", 128), ("x1bq", 1), ("x1bk", 1),
    ("b_w1", 512), ("b_w2", 512), ("b_cw", 12), ("b_cb", 4),
    ("r_k", 128), ("r_v", 128), ("r_r", 128), ("r_o", 128), ("r_mk", 1), ("r_mv", 1), ("r_mr", 1),
    ("r_td", 1), ("r_tf", 1),
    ("x2q", 128), ("x2k", 128), ("x2v", 128), ("x2o", 128),
    ("q_g", 384), ("q_u", 384), ("q_d", 352),
    ("a3q", 128), ("a3k", 128), ("a3v", 128), ("a3o", 128), ("a3bq", 1), ("a3bk", 1),
    ("x3q", 128), ("x3k", 128), ("x3v", 128),
    ("u_r", 64),
]
ROWS = [("ones", 128), ("a0bv", 128), ("a0bo", 128), ("f_bq", 256), ("f_bk", 256), ("f_bv", 256),
        ("x1bv", 128), ("a3bv", 128), ("a3bo", 128)]


def offsets(spec):
    at, out = 0, {}
    for name, width in spec:
        out[name] = (at, width)
        at += width
    return out, at


COL_AT, WCOLS = offsets(COLS)
ROW_AT, RCOLS = offsets(ROWS)


class Steps:

    def __init__(self, eng, sem):
        self.eng, self.sem, self.n = eng, sem, 0

    def mark(self, ins):
        ins.then_inc(self.sem, 1)
        self.n += 1
        return ins

    def wait(self):
        if self.n:
            self.eng.wait_ge(self.sem, self.n)

    def after(self, ins):
        self.mark(ins)
        self.wait()
        return ins


class Program:

    def __init__(self, nc, ctx):
        self.nc, self.ctx = nc, ctx
        self.used = []
        self.old = None
        self.stage = 0

    def sb(self, name, shape, dt=F32):
        return self.ctx.enter_context(self.nc.sbuf_tensor(name, shape, dt))

    def col(self, name):
        at, width = COL_AT[name]
        return self.w[:, at:at + width]

    def row(self, name):
        at, width = ROW_AT[name]
        return self.rows[0:1, at:at + width]

    def open(self, names):
        ctx = ExitStack()
        sems = {n: ctx.enter_context(self.nc.semaphore(f"s{self.stage}_{n}")) for n in names.split()}
        self.stage += 1
        clear, self.used = self.used, list(sems.values())
        old, self.old = self.old, ctx
        return sems, clear, old


def clear_sems(block, clear):
    @block.gpsimd
    def _(pool):
        for s in clear:
            pool.sem_clear(s)


def seq3(ap):
    return ap.rearrange("p (s t) -> p s t", t=SEQ)


def norm_stage(nc, P, last=False):
    S, clear, old = P.open("dve act var rstd normed turned copied")
    x = P.x_all[:] if last else P.x_tok[:].rearrange("p c t d -> p (c t) d")
    nt = x.shape[1]
    with nc.sbuf_tensor(f"n_st{P.stage}", [128, nt, 6], F32) as st, \
            nc.sbuf_tensor(f"n_mv{P.stage}", [128, nt, 2], F32) as mv, \
            nc.sbuf_tensor(f"n_w{P.stage}", [128, 4, nt], F32) as w, nc.Block() as block:
        clear_sems(block, clear)
        ve, y, t1, lnv = w[:, 0], w[:, 1], w[:, 2], w[:, 3]

        @block.vector
        def _(dve):
            own = Steps(dve, S["dve"])
            for t in range(nt):
                own.mark(nc.vector.bn_stats(st[:, t], x[:, t]))
            own.wait()
            for t in range(nt):
                own.mark(nc.vector.bn_aggr(mv[:, t], st[:, t]))
            own.wait()
            nc.vector.tensor_scalar(ve, mv[:, :, 1], EPS, None, ALU.add).then_inc(S["var"], 1)
            dve.wait_ge(S["var"], 1)
            dve.wait_ge(S["rstd"], 2)
            own.after(nc.vector.tensor_tensor(t1, y, y, ALU.mult))
            own.after(nc.vector.tensor_tensor(t1, t1, ve, ALU.mult))
            own.after(nc.vector.tensor_scalar(t1, t1, -0.5, 1.5, ALU.mult, ALU.add))
            own.after(nc.vector.tensor_tensor(y, y, t1, ALU.mult))
            for t in range(nt):
                nc.vector.tensor_scalar(x[:, t], x[:, t], mv[:, t, 0:1], y[:, t:t + 1],
                                        ALU.subtract, ALU.mult).then_inc(S["normed"], 1)

        @block.scalar
        def _(act):
            act.wait_ge(S["var"], 1)
            nc.scalar.activation(lnv, ve, ACT.Ln).then_inc(S["rstd"], 1)
            act.wait_ge(S["rstd"], 1)
            nc.scalar.activation(y, lnv, ACT.Exp, scale=-0.5).then_inc(S["rstd"], 1)
            if not last:
                for c in range(CHUNKS):
                    act.wait_ge(S["turned"], c + 1)
                    nc.scalar.copy(P.x_feat[:, c], P.ps[:, c]).then_inc(S["copied"], 1)

        if not last:
            @block.tensor
            def _(pe):
                for c in range(CHUNKS):
                    for t in range(TILES):
                        pe.wait_ge(S["normed"], c * TILES + t + 1)
                        mm = nc.tensor.transpose(P.ps[:, c, t * 128:(t + 1) * 128], P.x_tok[:, c, t],
                                                 P.col("ident"))
                    mm.then_inc(S["turned"], 1)
    if old:
        old.close()


def attention_stage(nc, P, wq, wk, wv, kv, bq=None, bk=None, bv=None, rope=None, mask=None,
                    kind="softmax", relu=False, wo=None, bo=None):
    S, clear, old = P.open("dve act qk v q_out k_out v_out_dve v_out_act scored shifted expd turned "
                           "turned_out summed normed att_turned att_out projected added")
    UN = 2 * TILES
    scale = float(HD) ** -0.5
    soft = kind == "softmax"
    QB, KB, SB, TB, OB = 0, 1, 2, 4, 6
    with ExitStack() as ctx:
        def sb(name, shape, dt=F32):
            return ctx.enter_context(nc.sbuf_tensor(f"{name}{P.stage}", shape, dt))
        q_sb = sb("t_q", [128, CHUNK])
        k_sb = sb("t_k", [128, 4, CHUNK])
        rot = sb("t_rot", [128, 2, CHUNK]) if rope else None
        mx = sb("t_mx", [128, 2, 8])
        prob = sb("t_p", [128, 2, 512])
        prob_t = sb("t_pt", [128, 2, 512])
        rden = sb("t_rd", [128, TILES, HEADS])
        att = sb("t_att", [128, TILES, HEADS, HD])
        att_t = sb("t_attt", [128, CHUNK]) if wo else None
        block = ctx.enter_context(nc.Block())
        clear_sems(block, clear)
        ps = P.ps
        o_ps = ps[:, OB:OB + 2].rearrange("p b (h c) -> p (b h) c", h=2)

        @block.tensor
        def _(pe):
            def project(c):
                if c >= 1:
                    pe.wait_ge(S["normed"], 2 * c)
                    pe.wait_ge(S["shifted"] if soft else S["expd"], UN * c)
                    pe.wait_ge(S["added"], c)
                xf = P.x_feat[:, c]
                kvf = kv[:, c]
                nc.tensor.matmul(ps[:, QB], P.col(wq), xf, start=True, stop=True)
                if rope:
                    nc.tensor.matmul(ps[:, SB], P.col(rope[0]), xf, start=True, stop=True)
                nc.tensor.matmul(ps[:, KB], P.col(wk), kvf, start=True, stop=True).then_inc(S["qk"], 1)
                for s in range(CSEQ):
                    for half in range(2):
                        out = ps[64 * half:64 * half + 64, OB + s // 4, (s % 4) * 128:(s % 4) * 128 + 128]
                        mm = nc.tensor.matmul(out, kvf[:, s * SEQ:(s + 1) * SEQ], P.col(wv),
                                              start=True, stop=not bv)
                        if bv:
                            mm = nc.tensor.matmul(out, P.row("ones")[:, 0:64], P.row(bv),
                                                  start=False, stop=True)
                mm.then_inc(S["v"], 1)

            def scores(c, u):
                n, tp, j = UN * c + u, u // 4, u % 4
                if n >= 2:
                    pe.wait_ge(S["shifted"] if soft else S["expd"], n - 1)
                if u == 0:
                    pe.wait_ge(S["q_out"], c + 1)
                    pe.wait_ge(S["k_out"], 4 * (c + 1))
                bank = ps[:, SB + n % 2]
                if mask == "causal":
                    nc.tensor.matmul(bank, P.ident_bf[:], P.causal8[:], start=True, stop=True)
                elif mask == "keys":
                    for i in range(2):
                        t = 2 * tp + i
                        nc.tensor.matmul(bank[:, 256 * i:256 * i + 256], P.sel_bf[0:CSEQ, t * 128:(t + 1) * 128],
                                         P.keys8[0:CSEQ, c, 0:256], start=(i == 0), stop=True,
                                         skip_group_check=True)
                r = 32 * j
                for i in range(2):
                    for half in range(2):
                        s = 2 * (2 * tp + i) + half
                        mm = nc.tensor.matmul(bank[64 * half:64 * half + 64, 256 * i:256 * i + 256],
                                              q_sb[r:r + 32, s * SEQ:(s + 1) * SEQ],
                                              k_sb[r:r + 32, :, s * SEQ:(s + 1) * SEQ],
                                              start=not mask, stop=True, skip_group_check=True,
                                              tile_position=(r, 64 * half))
                mm.then_inc(S["scored"], 1)

            def turn(c, u):
                n = UN * c + u
                pe.wait_ge(S["expd"], n + 1)
                if n >= 2:
                    pe.wait_ge(S["turned_out"], n - 1)
                for j in range(4):
                    mm = nc.tensor.transpose(ps[:, TB + n % 2, 128 * j:128 * j + 128],
                                             prob[:, n % 2, 128 * j:128 * j + 128], P.col("ident"))
                mm.then_inc(S["turned"], 1)

            def weigh(c, u):
                n, tp, j = UN * c + u, u // 4, u % 4
                pe.wait_ge(S["turned_out"], n + 1)
                if u == 0:
                    pe.wait_ge(S["v_out_dve"], 2 * (c + 1))
                    pe.wait_ge(S["v_out_act"], 2 * (c + 1))
                for half in range(2):
                    for i in range(4):
                        t, hp = 2 * tp + i // 2, 2 * j + i % 2
                        mm = nc.tensor.matmul(
                            o_ps[64 * half:64 * half + 64, t, 18 * hp:18 * hp + 18],
                            prob_t[:, n % 2, 128 * i + 64 * half:128 * i + 64 * half + 64],
                            P.v_pairs[:, 2 * t + half, hp], start=True, stop=True)
                mm.then_inc(S["summed"], 1)

            for c in range(CHUNKS):
                project(c)
                for u in range(UN + 2):
                    if u < UN:
                        scores(c, u)
                    if 1 <= u <= UN:
                        turn(c, u - 1)
                    if u >= 2:
                        weigh(c, u - 2)
                if wo:
                    pe.wait_ge(S["normed"], 2 * (c + 1))
                    for t in range(TILES):
                        mm = nc.tensor.transpose(ps[:, KB, t * 128:(t + 1) * 128],
                                                 att[:, t].rearrange("p h d -> p (h d)"), P.col("ident"))
                    mm.then_inc(S["att_turned"], 1)
                    pe.wait_ge(S["att_out"], c + 1)
                    for t in range(TILES):
                        out = ps[:, QB, t * 128:(t + 1) * 128]
                        mm = nc.tensor.matmul(out, att_t[:, t * 128:(t + 1) * 128], P.col(wo),
                                              start=True, stop=not bo)
                        if bo:
                            mm = nc.tensor.matmul(out, P.row("ones"), P.row(bo), start=False, stop=True)
                    mm.then_inc(S["projected"], 1)

        def v_part(half, bank, c):
            r = slice(64 * half, 64 * half + 64)
            src = ps[r, OB + bank].rearrange("p (s w e d) -> p (s w) e d", s=4, w=8, e=2)[:, :, half]
            dst = P.v_pairs[r, 4 * bank:4 * bank + 4].rearrange("p s w c -> p (s w) c")
            return dst[:, :, 9 * half:9 * half + 8], src

        @block.vector
        def _(dve):
            own = Steps(dve, S["dve"])
            for c in range(CHUNKS):
                dve.wait_ge(S["qk"], c + 1)
                k_src = ps[:, KB]
                if rope:
                    own.mark(nc.vector.tensor_scalar(rot[:, 0], ps[:, QB], P.col(bq), P.col("cosr"),
                                                     ALU.add, ALU.mult))
                    own.after(nc.vector.tensor_scalar(rot[:, 1], ps[:, SB], P.col(rope[1]), P.col("sinr"),
                                                      ALU.add, ALU.mult))
                    nc.vector.tensor_tensor(q_sb[:], rot[:, 0], rot[:, 1], ALU.add).then_inc(S["q_out"], 1)
                    dve.wait_ge(S["q_out"], c + 1)
                for s in range(4):
                    head = P.col("head4")[:, s:s + 1]
                    if not (bk or relu):
                        k_op = nc.vector.tensor_scalar(k_sb[:, s], k_src, head, None, ALU.mult)
                    elif relu:
                        k_op = nc.vector.tensor_scalar(k_sb[:, s], k_src, 0.0, head, ALU.max, ALU.mult)
                    else:
                        k_op = nc.vector.tensor_scalar(k_sb[:, s], k_src, P.col(bk), head,
                                                       ALU.add, ALU.mult)
                    k_op.then_inc(S["k_out"], 1)
                dve.wait_ge(S["v"], c + 1)
                for bank in range(2):
                    dst, src = v_part(0, bank, c)
                    if relu:
                        v_op = nc.vector.tensor_scalar(dst, src, 0.0, None, ALU.max)
                    else:
                        v_op = nc.vector.tensor_copy(dst, src)
                    v_op.then_inc(S["v_out_dve"], 1)
                if soft:
                    for u in range(UN):
                        n = UN * c + u
                        dve.wait_ge(S["scored"], n + 1)
                        sc = ps[:, SB + n % 2].rearrange("p (h k) -> p h k", k=SEQ)
                        own.after(nc.vector.tensor_reduce(mx[:, n % 2], sc, AX.X, ALU.max))
                        if n >= 2:
                            dve.wait_ge(S["turned"], n - 1)
                        nc.vector.tensor_tensor(
                            prob[:, n % 2].rearrange("p (h k) -> p h k", k=SEQ), sc,
                            mx[:, n % 2].rearrange("p (h o) -> p h o", o=1).to_broadcast([128, 8, SEQ]),
                            ALU.subtract).then_inc(S["shifted"], 1)
                for b in range(2):
                    dve.wait_ge(S["summed"], UN * c + 4 * (b + 1))
                    ts = slice(2 * b, 2 * b + 2)
                    o9 = o_ps[:, ts, 0:144].rearrange("p t (h c) -> p t h c", c=9)
                    if soft:
                        own.after(nc.vector.reciprocal(rden[:, ts], o9[:, :, :, 8]))
                        for t in range(2):
                            op = nc.vector.tensor_tensor(
                                att[:, 2 * b + t], o9[:, t, :, 0:8],
                                rden[:, 2 * b + t].rearrange("p (h o) -> p h o", o=1)
                                .to_broadcast([128, HEADS, HD]), ALU.mult)
                            if t == 0:
                                own.mark(op)
                        op.then_inc(S["normed"], 1)
                    else:
                        for t in range(2):
                            op = nc.vector.tensor_copy(att[:, 2 * b + t], o9[:, t, :, 0:8])
                            if t == 0:
                                own.mark(op)
                        op.then_inc(S["normed"], 1)
                xc = P.x_tok[:, c].rearrange("p t d -> p (t d)")
                if wo:
                    dve.wait_ge(S["projected"], c + 1)
                    y = ps[:, QB]
                else:
                    own.wait()
                    dve.wait_ge(S["normed"], 2 * (c + 1))
                    y = att[:].rearrange("p t h d -> p (t h d)")
                nc.vector.tensor_tensor(xc, xc, y, ALU.add).then_inc(S["added"], 1)
                if not wo:
                    dve.wait_ge(S["added"], c + 1)

        @block.scalar
        def _(act):
            for c in range(CHUNKS):
                act.wait_ge(S["qk"], c + 1)
                if not rope:
                    if relu:
                        q_op = nc.scalar.activation(q_sb[:], ps[:, QB], ACT.Relu)
                    elif bq:
                        q_op = nc.scalar.activation(q_sb[:], ps[:, QB], ACT.Identity, bias=P.col(bq))
                    else:
                        q_op = nc.scalar.copy(q_sb[:], ps[:, QB])
                    q_op.then_inc(S["q_out"], 1)
                act.wait_ge(S["v"], c + 1)
                for bank in range(2):
                    dst, src = v_part(1, bank, c)
                    v_op = nc.scalar.activation(dst, src, ACT.Relu if relu else ACT.Copy)
                    v_op.then_inc(S["v_out_act"], 1)
                for u in range(UN + 1):
                    n = UN * c + u
                    if u < UN:
                        if soft:
                            act.wait_ge(S["shifted"], n + 1)
                            op = nc.scalar.activation(prob[:, n % 2], prob[:, n % 2], ACT.Exp, scale=scale)
                        else:
                            act.wait_ge(S["scored"], n + 1)
                            if n >= 2:
                                act.wait_ge(S["turned"], n - 1)
                            op = nc.scalar.activation(prob[:, n % 2], ps[:, SB + n % 2], ACT.Sigmoid,
                                                      scale=scale)
                        op.then_inc(S["expd"], 1)
                    if u >= 1:
                        act.wait_ge(S["turned"], n)
                        if n >= 3:
                            act.wait_ge(S["summed"], n - 2)
                        nc.scalar.copy(prob_t[:, (n - 1) % 2], ps[:, TB + (n - 1) % 2])\
                            .then_inc(S["turned_out"], 1)
                if wo:
                    act.wait_ge(S["att_turned"], c + 1)
                    nc.scalar.copy(att_t[:], ps[:, KB]).then_inc(S["att_out"], 1)
    if old:
        old.close()


def quaternion_stage(nc, P):
    S, clear, old = P.open("dve act proj split freq freq_out mixed back added")
    with ExitStack() as ctx:
        def sb(name, shape, dt=F32):
            return ctx.enter_context(nc.sbuf_tensor(name, shape, dt))
        parts = sb("f_parts", [128, 2, 2, TILES, 128])
        mats = sb("f_mats", [128, 2, 3, 4, TILES * 32])
        prod = sb("f_prod", [128, 2, 4, TILES * 32])
        tmp = sb("f_tmp", [128, 4, 4, TILES * 32])
        comb = sb("f_comb", [128, 2, 4, TILES * 32])
        block = ctx.enter_context(nc.Block())
        clear_sems(block, clear)
        ps = P.ps

        @block.tensor
        def _(pe):
            for c in range(CHUNKS):
                for m, (w, b, src) in enumerate((("f_q", "f_bq", P.x_feat), ("f_k", "f_bk", P.ctx_feat),
                                                 ("f_v", "f_bv", P.ctx_feat))):
                    n = 3 * c + m
                    if n >= 1:
                        pe.wait_ge(S["split"], 2 * n)
                    for t in range(TILES):
                        out = ps[:, t // 2, (t % 2) * 256:(t % 2) * 256 + 256]
                        nc.tensor.matmul(out, src[:, c, t * 128:(t + 1) * 128], P.col(w),
                                         start=True, stop=False)
                        mm = nc.tensor.matmul(out, P.row("ones"), P.row(b), start=False, stop=True)
                    mm.then_inc(S["proj"], 1)
                    pe.wait_ge(S["split"], 2 * (n + 1))
                    even = parts[:, n % 2, 0].rearrange("p t f -> p (t f)")
                    odd = parts[:, n % 2, 1].rearrange("p t f -> p (t f)")
                    if n >= 2:
                        pe.wait_ge(S["freq_out"], 2 * (n - 1))
                    re, im = ps[:, 2 + 2 * (n % 2)], ps[:, 3 + 2 * (n % 2)]
                    nc.tensor.matmul(re, P.col("dft_c"), even, start=True, stop=False)
                    nc.tensor.matmul(re, P.col("dft_nd"), odd, start=False, stop=True)
                    nc.tensor.matmul(im, P.col("dft_d"), even, start=True, stop=False)
                    nc.tensor.matmul(im, P.col("dft_c"), odd, start=False, stop=True)\
                        .then_inc(S["freq"], 1)
                pe.wait_ge(S["mixed"], c + 1)
                if c >= 1:
                    pe.wait_ge(S["added"], c)
                out = ps[:, 6]
                nc.tensor.matmul(out, P.col("inv_c"), comb[:, 0].rearrange("p i x -> p (i x)"),
                                 start=True, stop=False)
                nc.tensor.matmul(out, P.col("inv_ns"), comb[:, 1].rearrange("p i x -> p (i x)"),
                                 start=False, stop=True).then_inc(S["back"], 1)

        @block.scalar
        def _(act):
            for n in range(3 * CHUNKS):
                act.wait_ge(S["freq"], n + 1)
                if n >= 3:
                    act.wait_ge(S["mixed"], n // 3)
                for ri in range(2):
                    bank = ps[:, 2 + 2 * (n % 2) + ri].rearrange("p (t i x) -> p i t x", t=TILES, i=4)
                    dst = mats[:, ri, n % 3].rearrange("p i (t x) -> p i t x", t=TILES)
                    nc.scalar.copy(dst, bank).then_inc(S["freq_out"], 1)

        @block.vector
        def _(dve):
            own = Steps(dve, S["dve"])

            def quad(ap):
                return ap.rearrange("p (i j) x -> p i j x", i=2)

            def matmul2(ar, ai, br, bi, out):
                shape = [128, 2, 2, TILES * 32]

                def term(a, b, k, slot):
                    lhs = quad(a)[:, :, k:k + 1].to_broadcast(shape)
                    rhs = quad(b)[:, k:k + 1].to_broadcast(shape)
                    own.mark(nc.vector.tensor_tensor(quad(tmp[:, slot]), lhs, rhs, ALU.mult))
                for ri, (a1, b1, a2, b2, op) in enumerate(((ar, br, ai, bi, ALU.subtract),
                                                           (ar, bi, ai, br, ALU.add))):
                    own.wait()
                    term(a1, b1, 0, 0)
                    term(a1, b1, 1, 1)
                    term(a2, b2, 0, 2)
                    term(a2, b2, 1, 3)
                    own.wait()
                    own.mark(nc.vector.tensor_tensor(tmp[:, 0], tmp[:, 0], tmp[:, 1], ALU.add))
                    own.after(nc.vector.tensor_tensor(tmp[:, 2], tmp[:, 2], tmp[:, 3], ALU.add))
                    own.mark(nc.vector.tensor_tensor(out[ri], tmp[:, 0], tmp[:, 2], op))
                own.wait()

            sign = P.col("sign").rearrange("p (e f) -> p e f", e=2)
            for c in range(CHUNKS):
                for m in range(3):
                    n = 3 * c + m
                    dve.wait_ge(S["proj"], n + 1)
                    if n >= 2:
                        dve.wait_ge(S["freq"], n - 1)
                    for b in range(2):
                        src = ps[:, b].rearrange("p (t e f) -> p e t f", t=2, e=2)
                        for e in range(2):
                            op = nc.vector.tensor_tensor(
                                parts[:, n % 2, e, 2 * b:2 * b + 2], src[:, e],
                                sign[:, e:e + 1].to_broadcast([128, 2, 128]), ALU.mult)
                            if e == 0:
                                own.mark(op)
                        op.then_inc(S["split"], 1)
                    own.wait()
                dve.wait_ge(S["freq_out"], 6 * (c + 1))
                A = [[mats[:, ri, m] for ri in range(2)] for m in range(3)]
                matmul2(A[0][0], A[0][1], A[1][0], A[1][1], [prod[:, 0], prod[:, 1]])
                matmul2(prod[:, 0], prod[:, 1], A[2][0], A[2][1], A[0])
                re, im = A[0]
                if c >= 1:
                    dve.wait_ge(S["back"], c)
                V = nc.vector
                own.mark(V.tensor_tensor(comb[:, 0, 0], re[:, 0], re[:, 3], ALU.add))
                own.mark(V.tensor_tensor(comb[:, 1, 0], im[:, 0], im[:, 3], ALU.add))
                own.mark(V.tensor_tensor(comb[:, 0, 1], im[:, 0], im[:, 3], ALU.subtract))
                own.mark(V.tensor_tensor(comb[:, 1, 1], re[:, 3], re[:, 0], ALU.subtract))
                own.mark(V.tensor_tensor(comb[:, 0, 2], re[:, 1], re[:, 2], ALU.subtract))
                own.mark(V.tensor_tensor(comb[:, 1, 2], im[:, 1], im[:, 2], ALU.subtract))
                own.mark(V.tensor_tensor(comb[:, 0, 3], im[:, 1], im[:, 2], ALU.add))
                own.after(V.scalar_tensor_tensor(out=comb[:, 1, 3], in0=re[:, 1], scalar=-1.0, in1=re[:, 2],
                                                 op0=ALU.mult, op1=ALU.subtract))
                V.tensor_copy(tmp[:, 0, 0, 0:1], comb[:, 1, 3, 0:1]).then_inc(S["mixed"], 1)
                dve.wait_ge(S["back"], c + 1)
                dve.wait_ge(S["mixed"], c + 1)
                y = ps[:, 6].rearrange("p (i t x) -> p t i x", i=4, t=TILES)
                xc = P.x_tok[:, c].rearrange("p t (i x) -> p t i x", i=4)
                V.tensor_tensor(xc, xc, y, ALU.add).then_inc(S["added"], 1)
    if old:
        old.close()


def small_experts_stage(nc, P):
    S, clear, old = P.open("dve act logits chosen turned mask_out hid hid_out squared masked summed added")
    with ExitStack() as ctx:
        def sb(name, shape, dt=F32):
            return ctx.enter_context(nc.sbuf_tensor(name, shape, dt))
        mx = sb("e_mx", [128, 2, TILES])
        eq = sb("e_eq", [128, 3, TILES, NE8])
        one_t = sb("e_onet", [NE8, CHUNK], BF16)
        hid = sb("e_hid", [128, 2, CHUNK])
        act_h = sb("e_act", [128, 4, CHUNK])
        block = ctx.enter_context(nc.Block())
        clear_sems(block, clear)
        ps = P.ps

        @block.tensor
        def _(pe):
            for c in range(CHUNKS):
                if c >= 1:
                    pe.wait_ge(S["added"], c)
                for t in range(TILES):
                    mm = nc.tensor.matmul(ps[:, 0, NE8 * t:NE8 * t + NE8],
                                          P.x_feat[:, c, t * 128:(t + 1) * 128], P.col("m_r"),
                                          start=True, stop=True)
                mm.then_inc(S["logits"], 1)
                pe.wait_ge(S["chosen"], c + 1)
                for t in range(TILES):
                    mm = nc.tensor.transpose(ps[0:NE8, 1, t * 128:(t + 1) * 128], eq[:, 2, t],
                                             P.col("ident"))
                mm.then_inc(S["turned"], 1)
                for j in range(4):
                    n = 4 * c + j
                    if n >= 2:
                        pe.wait_ge(S["masked"], n - 1)
                    nc.tensor.matmul(ps[:, 2 + n % 2], P.col("m_fc")[:, 128 * j:128 * j + 128],
                                     P.x_feat[:, c], start=True, stop=True)
                    pe.wait_ge(S["mask_out"], c + 1)
                    nc.tensor.matmul(ps[:, 4 + n % 2], P.spread_bf[0:NE8, 128 * j:128 * j + 128],
                                     one_t[:], start=True, stop=True).then_inc(S["hid"], 1)
                pe.wait_ge(S["masked"], 4 * (c + 1))
                for t in range(TILES):
                    for j in range(4):
                        mm = nc.tensor.matmul(ps[:, 6, t * 128:(t + 1) * 128],
                                              act_h[:, j, t * 128:(t + 1) * 128],
                                              P.col("m_pj")[:, 128 * j:128 * j + 128],
                                              start=(j == 0), stop=(j == 3))
                mm.then_inc(S["summed"], 1)

        @block.scalar
        def _(act):
            for c in range(CHUNKS):
                act.wait_ge(S["turned"], c + 1)
                nc.scalar.copy(one_t[:], ps[0:NE8, 1]).then_inc(S["mask_out"], 1)
                for j in range(4):
                    n = 4 * c + j
                    act.wait_ge(S["hid"], n + 1)
                    if n >= 2:
                        act.wait_ge(S["masked"], n - 1)
                    nc.scalar.copy(hid[:, n % 2], ps[:, 2 + n % 2]).then_inc(S["hid_out"], 1)

        @block.vector
        def _(dve):
            own = Steps(dve, S["dve"])
            V = nc.vector
            for c in range(CHUNKS):
                dve.wait_ge(S["logits"], c + 1)
                lg = ps[:, 0, 0:NE8 * TILES].rearrange("p (t e) -> p t e", e=NE8)

                def wide(ap):
                    return ap.rearrange("p (t o) -> p t o", o=1).to_broadcast([128, TILES, NE8])
                own.after(V.tensor_reduce(mx[:, 0], lg, AX.X, ALU.max))
                own.after(V.tensor_tensor(eq[:, 0], lg, wide(mx[:, 0]), ALU.is_equal))
                own.after(V.tensor_tensor(eq[:, 1], eq[:, 0],
                                          P.col("desc8")[:, None, :].to_broadcast([128, TILES, NE8]), ALU.mult))
                own.after(V.tensor_reduce(mx[:, 1], eq[:, 1], AX.X, ALU.max))
                V.tensor_tensor(eq[:, 2], eq[:, 1], wide(mx[:, 1]), ALU.is_equal).then_inc(S["chosen"], 1)
                for j in range(4):
                    n = 4 * c + j
                    dve.wait_ge(S["hid_out"], n + 1)
                    h = hid[:, n % 2]
                    own.after(V.scalar_tensor_tensor(out=h, in0=h, scalar=0.5, in1=h, op0=ALU.mult, op1=ALU.max))
                    own.after(V.tensor_tensor(h, h, h, ALU.mult))
                    V.tensor_tensor(act_h[:, j], h, ps[:, 4 + n % 2], ALU.mult).then_inc(S["masked"], 1)
                dve.wait_ge(S["summed"], c + 1)
                xc = P.x_tok[:, c].rearrange("p t d -> p (t d)")
                V.tensor_tensor(xc, xc, ps[:, 6], ALU.add).then_inc(S["added"], 1)
    if old:
        old.close()


def gated_scan_stage(nc, P):
    S, clear, old = P.open("dve act proj gates scanned turned added")
    with ExitStack() as ctx:
        def sb(name, shape, dt=F32):
            return ctx.enter_context(nc.sbuf_tensor(name, shape, dt))
        keep = sb("g_keep", [128, CHUNK])
        take = sb("g_take", [128, CHUNK])
        cand = sb("g_cand", [128, CHUNK])
        state = sb("g_state", [128, 2, CHUNK])
        block = ctx.enter_context(nc.Block())
        clear_sems(block, clear)
        ps = P.ps

        @block.tensor
        def _(pe):
            def turn(c):
                pe.wait_ge(S["scanned"], c + 1)
                for t in range(TILES):
                    mm = nc.tensor.transpose(ps[:, 4 + c % 2, t * 128:(t + 1) * 128],
                                             state[:, c % 2, t * 128:(t + 1) * 128], P.col("ident"))
                mm.then_inc(S["turned"], 1)
            for c in range(CHUNKS):
                for j in range(2):
                    mm = nc.tensor.matmul(ps[:, 2 * (c % 2) + j], P.col("g_hg")[:, 128 * j:128 * j + 128],
                                          P.x_feat[:, c], start=True, stop=True)
                mm.then_inc(S["proj"], 1)
            for c in range(CHUNKS):
                turn(c)

        @block.scalar
        def _(act):
            for c in range(CHUNKS):
                act.wait_ge(S["proj"], c + 1)
                if c >= 1:
                    act.wait_ge(S["scanned"], c)
                hid, gate = ps[:, 2 * (c % 2)], ps[:, 2 * (c % 2) + 1]
                nc.scalar.activation(keep[:], gate, ACT.Sigmoid, scale=-1.0).then_inc(S["gates"], 1)
                nc.scalar.activation(take[:], gate, ACT.Sigmoid).then_inc(S["gates"], 1)
                nc.scalar.activation(cand[:], hid, ACT.Sigmoid).then_inc(S["gates"], 1)

        @block.vector
        def _(dve):
            own = Steps(dve, S["dve"])
            V = nc.vector
            for c in range(CHUNKS):
                dve.wait_ge(S["gates"], 3 * (c + 1))
                own.mark(V.memset(seq3(keep[:])[:, :, 0:1], 0.0))
                own.after(V.scalar_tensor_tensor(out=cand[:], in0=ps[:, 2 * (c % 2)], scalar=0.5,
                                                 in1=cand[:], op0=ALU.add, op1=ALU.max))
                own.after(V.tensor_tensor(take[:], take[:], cand[:], ALU.mult))
                V.tensor_tensor_scan(state[:, c % 2], keep[:], take[:], 0.0, ALU.mult, ALU.add)\
                    .then_inc(S["scanned"], 1)
                dve.wait_ge(S["scanned"], c + 1)
            for c in range(CHUNKS):
                dve.wait_ge(S["turned"], c + 1)
                xc = P.x_tok[:, c].rearrange("p t d -> p (t d)")
                V.tensor_tensor(xc, xc, ps[:, 4 + c % 2], ALU.add).then_inc(S["added"], 1)
    if old:
        old.close()


def bitnet_stage(nc, P):
    S, clear, old = P.open("dve act quant turned turned_out hid hid_out conved silued wide quant2 "
                           "back back_out projected added")
    nb = TILES
    with ExitStack() as ctx:
        def sb(name, shape, dt=F32):
            return ctx.enter_context(nc.sbuf_tensor(name, shape, dt))
        am = sb("b_am", [128, 3, nb])
        xq = sb("b_xq", [128, TILES, D])
        xq_t = sb("b_xqt", [128, CHUNK])
        hpad = P.hpad
        conv = sb("b_conv", [128, 4, CHUNK])
        hq = sb("b_hq", [128, 2, HID1])
        hq_t = sb("b_hqt", [128, 2, HID1])
        am2 = sb("b_am2", [128, 3])
        block = ctx.enter_context(nc.Block())
        clear_sems(block, clear)
        ps = P.ps

        @block.tensor
        def _(pe):
            for c in range(CHUNKS):
                pe.wait_ge(S["quant"], c + 1)
                if c >= 1:
                    pe.wait_ge(S["added"], c)
                for t in range(TILES):
                    mm = nc.tensor.transpose(ps[:, 0, t * 128:(t + 1) * 128], xq[:, t], P.col("ident"))
                mm.then_inc(S["turned"], 1)
                pe.wait_ge(S["turned_out"], c + 1)
                for j in range(4):
                    n = 4 * c + j
                    if n >= 2:
                        pe.wait_ge(S["hid_out"], n - 1)
                    nc.tensor.matmul(ps[:, 1 + n % 2], P.w1q[:, 128 * j:128 * j + 128], xq_t[:],
                                     start=True, stop=True).then_inc(S["hid"], 1)
                for t in range(TILES):
                    n = 4 * c + t
                    if t == 0:
                        pe.wait_ge(S["silued"], 4 * (c + 1))
                    if n >= 2:
                        pe.wait_ge(S["quant2"], n - 1)
                    for j in range(4):
                        mm = nc.tensor.transpose(ps[:, 3 + n % 2, 128 * j:128 * j + 128],
                                                 conv[:, j, t * 128:(t + 1) * 128], P.col("ident"))
                    mm.then_inc(S["wide"], 1)
                    pe.wait_ge(S["quant2"], n + 1)
                    if n >= 1:
                        pe.wait_ge(S["back_out"], n)
                    for j in range(4):
                        mm = nc.tensor.transpose(ps[:, 5, 128 * j:128 * j + 128],
                                                 hq[:, n % 2, 128 * j:128 * j + 128], P.col("ident"))
                    mm.then_inc(S["back"], 1)
                    pe.wait_ge(S["back_out"], n + 1)
                    for j in range(4):
                        mm = nc.tensor.matmul(ps[:, 6, t * 128:(t + 1) * 128],
                                              hq_t[:, n % 2, 128 * j:128 * j + 128],
                                              P.w2q[:, 128 * j:128 * j + 128], start=(j == 0), stop=(j == 3))
                mm.then_inc(S["projected"], 1)

        @block.scalar
        def _(act):
            for c in range(CHUNKS):
                act.wait_ge(S["turned"], c + 1)
                nc.scalar.copy(xq_t[:], ps[:, 0]).then_inc(S["turned_out"], 1)
                for j in range(4):
                    n = 4 * c + j
                    act.wait_ge(S["hid"], n + 1)
                    if c >= 1:
                        act.wait_ge(S["conved"], 4 * c)
                    nc.scalar.copy(hpad[:, j, :, 1:65], seq3(ps[:, 1 + n % 2])).then_inc(S["hid_out"], 1)
                for j in range(4):
                    n = 4 * c + j
                    act.wait_ge(S["conved"], n + 1)
                    nc.scalar.activation(conv[:, j], conv[:, j], ACT.Silu).then_inc(S["silued"], 1)
                for t in range(TILES):
                    n = 4 * c + t
                    act.wait_ge(S["back"], n + 1)
                    nc.scalar.copy(hq_t[:, n % 2], ps[:, 5]).then_inc(S["back_out"], 1)

        @block.vector
        def _(dve):
            own = Steps(dve, S["dve"])
            V = nc.vector

            def scales(amax, r, s, inv):
                own.after(V.tensor_scalar(r, amax, 1e-5, None, ALU.max))
                own.after(V.reciprocal(s, r))
                own.after(V.tensor_scalar(s, s, 127.0, None, ALU.mult))
                own.after(V.reciprocal(inv, s))

            for c in range(CHUNKS):
                if c >= 1:
                    dve.wait_ge(S["turned"], c)
                own.after(V.tensor_reduce(am[:, 0], P.x_tok[:, c], AX.X, ALU.max, apply_absolute_value=True))
                scales(am[:, 0], am[:, 0], am[:, 1], am[:, 2])

                def wide(ap):
                    return ap.rearrange("p (t o) -> p t o", o=1).to_broadcast([128, TILES, D])
                own.after(V.tensor_tensor(xq[:], P.x_tok[:, c], wide(am[:, 1]), ALU.mult))
                own.after(V.tensor_scalar(xq[:], xq[:], ROUND, -ROUND, ALU.add, ALU.add))
                own.after(V.tensor_scalar(xq[:], xq[:], 127.0, -128.0, ALU.min, ALU.max))
                V.tensor_tensor(xq[:], xq[:], wide(am[:, 2]), ALU.mult).then_inc(S["quant"], 1)
                cw, cb = P.col("b_cw"), P.col("b_cb")
                for j in range(4):
                    n = 4 * c + j
                    dve.wait_ge(S["hid_out"], n + 1)
                    if c >= 1:
                        dve.wait_ge(S["wide"], 4 * c)
                    y = seq3(conv[:, j])
                    own.after(V.tensor_scalar(y, hpad[:, j, :, 1:65], cw[:, 3 * j + 1:3 * j + 2],
                                              cb[:, j:j + 1], ALU.mult, ALU.add))
                    own.after(V.scalar_tensor_tensor(out=y, in0=hpad[:, j, :, 0:64], scalar=cw[:, 3 * j:3 * j + 1],
                                                     in1=y, op0=ALU.mult, op1=ALU.add))
                    V.scalar_tensor_tensor(out=y, in0=hpad[:, j, :, 2:66], scalar=cw[:, 3 * j + 2:3 * j + 3],
                                           in1=y, op0=ALU.mult, op1=ALU.add).then_inc(S["conved"], 1)
                for t in range(TILES):
                    n = 4 * c + t
                    dve.wait_ge(S["wide"], n + 1)
                    h = ps[:, 3 + n % 2]
                    own.after(V.tensor_reduce(am2[:, 0:1], h, AX.X, ALU.max, apply_absolute_value=True))
                    scales(am2[:, 0:1], am2[:, 0:1], am2[:, 1:2], am2[:, 2:3])
                    if n >= 2:
                        dve.wait_ge(S["back"], n - 1)
                    q = hq[:, n % 2]
                    own.after(V.tensor_scalar(q, h, am2[:, 1:2], ROUND, ALU.mult, ALU.add))
                    own.after(V.tensor_scalar(q, q, -ROUND, 127.0, ALU.add, ALU.min))
                    V.tensor_scalar(q, q, -128.0, am2[:, 2:3], ALU.max, ALU.mult).then_inc(S["quant2"], 1)
                    dve.wait_ge(S["quant2"], n + 1)
                dve.wait_ge(S["projected"], c + 1)
                xc = P.x_tok[:, c].rearrange("p t d -> p (t d)")
                V.tensor_tensor(xc, xc, ps[:, 6], ALU.add).then_inc(S["added"], 1)
    if old:
        old.close()


def rwkv_stage(nc, P):
    S, clear, old = P.open("dve act lerped proj k_out r_out arg1 e1b arg2 e2b arg3 e1 arg4 e2 read_v "
                           "mixed projected added")
    with ExitStack() as ctx:
        def sb(name, shape, dt=F32):
            return ctx.enter_context(nc.sbuf_tensor(name, shape, dt))
        prev = sb("r_prev", [128, CSEQ, SEQ])
        lerp = sb("r_lerp", [128, 3, CHUNK])
        tmp = sb("r_tmp", [128, 2, CHUNK])
        pp = sb("r_pp", [128, CSEQ, SEQ + 1])
        aa = sb("r_aa", [128, CSEQ, SEQ + 1])
        bb = sb("r_bb", [128, CSEQ, SEQ + 1])
        er = sb("r_er", [128, CHUNK])
        e1 = sb("r_e1", [128, CHUNK])
        e2 = sb("r_e2", [128, CHUNK])
        out = sb("r_out", [128, CHUNK])
        kp, e1b, e2b, ev = P.kpad, P.e1b, P.e2b, P.ev
        block = ctx.enter_context(nc.Block())
        clear_sems(block, clear)
        ps = P.ps

        def flat(t):
            return t[:].rearrange("p s t -> p (s t)")

        @block.tensor
        def _(pe):
            for c in range(CHUNKS):
                pe.wait_ge(S["lerped"], c + 1)
                if c >= 1:
                    pe.wait_ge(S["k_out"], c)
                    pe.wait_ge(S["r_out"], c)
                    pe.wait_ge(S["mixed"], c)
                for j, w in enumerate(("r_k", "r_v", "r_r")):
                    mm = nc.tensor.matmul(ps[:, j], P.col(w), lerp[:, j], start=True, stop=True)
                mm.then_inc(S["proj"], 1)
                pe.wait_ge(S["mixed"], c + 1)
                if c >= 1:
                    pe.wait_ge(S["added"], c)
                for t in range(TILES):
                    mm = nc.tensor.matmul(ps[:, 3, t * 128:(t + 1) * 128], out[:, t * 128:(t + 1) * 128],
                                          P.col("r_o"), start=True, stop=True)
                mm.then_inc(S["projected"], 1)

        @block.scalar
        def _(act):
            for c in range(CHUNKS):
                act.wait_ge(S["proj"], c + 1)
                if c >= 1:
                    act.wait_ge(S["mixed"], c)
                nc.scalar.copy(kp[:, :, 1:65], seq3(ps[:, 0])).then_inc(S["k_out"], 1)
                nc.scalar.activation(er[:], ps[:, 2], ACT.Exp, scale=-1.0).then_inc(S["r_out"], 1)
                act.wait_ge(S["arg1"], c + 1)
                nc.scalar.activation(e1b[:, :, 1:65], e1b[:, :, 1:65], ACT.Exp).then_inc(S["e1b"], 1)
                act.wait_ge(S["arg2"], c + 1)
                nc.scalar.activation(e2b[:, :, 1:65], e2b[:, :, 1:65], ACT.Exp).then_inc(S["e2b"], 1)
                act.wait_ge(S["arg3"], c + 1)
                nc.scalar.activation(e1[:], e1[:], ACT.Exp).then_inc(S["e1"], 1)
                act.wait_ge(S["arg4"], c + 1)
                nc.scalar.activation(e2[:], e2[:], ACT.Exp).then_inc(S["e2"], 1)

        @block.vector
        def _(dve):
            own = Steps(dve, S["dve"])
            V = nc.vector
            for c in range(CHUNKS):
                xs = seq3(P.x_feat[:, c])
                if c >= 1:
                    dve.wait_ge(S["proj"], c)
                own.mark(V.memset(prev[:, :, 0:1], 0.0))
                own.after(V.tensor_copy(prev[:, :, 1:64], xs[:, :, 0:63]))
                for j, m in enumerate(("r_mk", "r_mv", "r_mr")):
                    own.after(V.tensor_scalar(seq3(tmp[:, 0]), prev[:], P.one_minus[:, j:j + 1], None, ALU.mult))
                    op = V.scalar_tensor_tensor(out=seq3(lerp[:, j]), in0=xs, scalar=P.col(m),
                                                in1=seq3(tmp[:, 0]), op0=ALU.mult, op1=ALU.add)
                    if j < 2:
                        own.after(op)
                op.then_inc(S["lerped"], 1)
                dve.wait_ge(S["k_out"], c + 1)
                dve.wait_ge(S["lerped"], c + 1)
                own.after(V.tensor_tensor_scan(flat(pp), flat(P.decay), flat(kp), FIRST_PP, ALU.add, ALU.max))
                before, now, kt = pp[:, :, 0:64], pp[:, :, 1:65], kp[:, :, 1:65]
                V.scalar_tensor_tensor(out=e1b[:, :, 1:65], in0=before, scalar=P.w_dec[:, 0:1], in1=now,
                                       op0=ALU.add, op1=ALU.subtract).then_inc(S["arg1"], 1)
                V.tensor_tensor(e2b[:, :, 1:65], kt, now, ALU.subtract).then_inc(S["arg2"], 1)
                p = seq3(tmp[:, 1])
                own.after(V.scalar_tensor_tensor(out=p, in0=kt, scalar=P.col("r_tf"), in1=before,
                                                 op0=ALU.add, op1=ALU.max))
                V.tensor_tensor(seq3(e1[:]), before, p, ALU.subtract).then_inc(S["arg3"], 1)
                V.scalar_tensor_tensor(out=seq3(e2[:]), in0=kt, scalar=P.col("r_tf"), in1=p,
                                       op0=ALU.add, op1=ALU.subtract).then_inc(S["arg4"], 1)
                dve.wait_ge(S["e1b"], c + 1)
                dve.wait_ge(S["e2b"], c + 1)
                own.mark(V.tensor_tensor_scan(flat(bb), flat(e1b), flat(e2b), 0.0, ALU.mult, ALU.add))
                own.after(V.tensor_tensor(ev[:, :, 1:65], e2b[:, :, 1:65], seq3(ps[:, 1]), ALU.mult))
                own.after(V.tensor_tensor_scan(flat(aa), flat(e1b), flat(ev), 0.0, ALU.mult, ALU.add))
                dve.wait_ge(S["e1"], c + 1)
                dve.wait_ge(S["e2"], c + 1)
                num, den = tmp[:, 0], tmp[:, 1]
                own.mark(V.tensor_tensor(seq3(num), seq3(e1[:]), aa[:, :, 0:64], ALU.mult))
                own.mark(V.tensor_tensor(seq3(den), seq3(e1[:]), bb[:, :, 0:64], ALU.mult))
                own.after(V.tensor_tensor(out[:], e2[:], ps[:, 1], ALU.mult))
                own.mark(V.tensor_tensor(num, num, out[:], ALU.add))
                own.after(V.tensor_tensor(den, den, e2[:], ALU.add))
                dve.wait_ge(S["r_out"], c + 1)
                own.after(V.scalar_tensor_tensor(out=den, in0=er[:], scalar=1.0, in1=den,
                                                 op0=ALU.add, op1=ALU.mult))
                own.after(V.reciprocal(den, den))
                V.tensor_tensor(out[:], num, den, ALU.mult).then_inc(S["mixed"], 1)
                dve.wait_ge(S["mixed"], c + 1)
                dve.wait_ge(S["projected"], c + 1)
                xc = P.x_tok[:, c].rearrange("p t d -> p (t d)")
                V.tensor_tensor(xc, xc, ps[:, 3], ALU.add).then_inc(S["added"], 1)
    if old:
        old.close()


def fp4_steps(nc, own, src, out, ax, mag, amax, inv, nblk, scale_sem=None):
    V = nc.vector

    def blocks(ap):
        return ap.rearrange("p (b w) -> p b w", w=BLK)

    def wide(ap):
        return ap.rearrange("p (b o) -> p b o", o=1).to_broadcast([ap.shape[0], nblk, BLK])
    own.after(V.tensor_reduce(amax, blocks(src), AX.X, ALU.max, apply_absolute_value=True))
    own.after(V.tensor_scalar(amax, amax, 1.0 / 6.0, 1e-12, ALU.mult, ALU.max))
    own.after(V.reciprocal(inv, amax))
    own.after(V.tensor_tensor(blocks(out), blocks(src), wide(inv), ALU.mult))
    own.after(V.scalar_tensor_tensor(out=ax, in0=out, scalar=-1.0, in1=out, op0=ALU.mult, op1=ALU.max))
    own.after(V.tensor_scalar(mag, ax, 5.0, 2.0, ALU.is_gt, ALU.mult))
    own.after(V.scalar_tensor_tensor(out=mag, in0=ax, scalar=3.5, in1=mag, op0=ALU.is_gt, op1=ALU.add))
    own.after(V.scalar_tensor_tensor(out=mag, in0=ax, scalar=2.5, in1=mag, op0=ALU.is_gt, op1=ALU.add))
    own.after(V.tensor_scalar(mag, mag, 2.0, None, ALU.mult))
    for mid in (1.75, 1.25, 0.75, 0.25):
        own.after(V.scalar_tensor_tensor(out=mag, in0=ax, scalar=mid, in1=mag, op0=ALU.is_gt, op1=ALU.add))
    own.after(V.tensor_scalar(ax, out, 0.0, -0.5, ALU.is_gt, ALU.add))
    own.after(V.tensor_tensor(mag, mag, ax, ALU.mult))
    return V.tensor_tensor(blocks(out), blocks(mag), wide(amax), ALU.mult)


def fp4_stage(nc, P):
    S, clear, old = P.open("dve act quant turned turned_out gate silued hq back back_out projected added")
    NI = 3
    with ExitStack() as ctx:
        def sb(name, shape, dt=F32):
            return ctx.enter_context(nc.sbuf_tensor(name, shape, dt))
        xq = sb("q_xq", [128, CHUNK])
        ax = sb("q_ax", [128, CHUNK])
        mag = sb("q_mag", [128, CHUNK])
        am = sb("q_am", [128, 2, 32])
        xq_t = sb("q_xqt", [128, CHUNK])
        h = sb("q_h", [128, 2, I2])
        hq = sb("q_hq", [128, 2, I2])
        hq_t = sb("q_hqt", [128, 2, NI * 128])
        block = ctx.enter_context(nc.Block())
        clear_sems(block, clear)
        ps = P.ps

        @block.tensor
        def _(pe):
            for c in range(CHUNKS):
                pe.wait_ge(S["quant"], c + 1)
                for t in range(TILES):
                    mm = nc.tensor.transpose(ps[:, 0, t * 128:(t + 1) * 128], xq[:, t * 128:(t + 1) * 128],
                                             P.col("ident"))
                mm.then_inc(S["turned"], 1)
                pe.wait_ge(S["turned_out"], c + 1)

                def gate_up(t):
                    n = 4 * c + t
                    if n >= 2:
                        pe.wait_ge(S["hq"], n - 1)
                    xt = xq_t[:, t * 128:(t + 1) * 128]
                    nc.tensor.matmul(ps[:, 1 + n % 2, 0:I2], xt, P.gate_q[:], start=True, stop=True)
                    nc.tensor.matmul(ps[:, 3 + n % 2, 0:I2], xt, P.up_q[:], start=True, stop=True)\
                        .then_inc(S["gate"], 1)

                gate_up(0)
                for t in range(TILES):
                    n = 4 * c + t
                    if t + 1 < TILES:
                        gate_up(t + 1)
                    pe.wait_ge(S["hq"], n + 1)
                    if n >= 1:
                        pe.wait_ge(S["back_out"], n)
                    for j in range(NI):
                        w = min(128, I2 - 128 * j)
                        mm = nc.tensor.transpose(ps[0:w, 5, 128 * j:128 * j + 128],
                                                 hq[:, n % 2, 128 * j:128 * j + w], P.col("ident"))
                    mm.then_inc(S["back"], 1)
                    pe.wait_ge(S["back_out"], n + 1)
                    if t == 0 and c >= 1:
                        pe.wait_ge(S["added"], c)
                    for j in range(NI):
                        w = min(128, I2 - 128 * j)
                        mm = nc.tensor.matmul(ps[:, 6, t * 128:(t + 1) * 128],
                                              hq_t[0:w, n % 2, 128 * j:128 * j + 128],
                                              P.down_q[0:w, 128 * j:128 * j + 128],
                                              start=(j == 0), stop=(j == NI - 1))
                mm.then_inc(S["projected"], 1)

        @block.scalar
        def _(act):
            own = Steps(act, S["act"])
            for c in range(CHUNKS):
                act.wait_ge(S["turned"], c + 1)
                nc.scalar.copy(xq_t[:], ps[:, 0]).then_inc(S["turned_out"], 1)

                def silu(t):
                    n = 4 * c + t
                    act.wait_ge(S["gate"], n + 1)
                    if n >= 2:
                        act.wait_ge(S["hq"], n - 1)
                    nc.scalar.activation(h[:, n % 2], ps[:, 1 + n % 2, 0:I2], ACT.Silu).then_inc(S["silued"], 1)
                silu(0)
                for t in range(TILES):
                    n = 4 * c + t
                    if t + 1 < TILES:
                        silu(t + 1)
                    act.wait_ge(S["back"], n + 1)
                    own.mark(nc.scalar.copy(hq_t[:, n % 2, 0:256], ps[:, 5, 0:256]))
                    nc.scalar.copy(hq_t[0:96, n % 2, 256:384], ps[0:96, 5, 256:384]).then_inc(S["back_out"], 1)

        @block.vector
        def _(dve):
            own = Steps(dve, S["dve"])
            V = nc.vector
            for c in range(CHUNKS):
                if c >= 1:
                    dve.wait_ge(S["turned"], c)
                src = P.x_tok[:, c].rearrange("p t d -> p (t d)")
                fp4_steps(nc, own, src, xq[:], ax[:], mag[:], am[:, 0], am[:, 1], 32)\
                    .then_inc(S["quant"], 1)
                dve.wait_ge(S["quant"], c + 1)
                for t in range(TILES):
                    n = 4 * c + t
                    dve.wait_ge(S["silued"], n + 1)
                    if n >= 2:
                        dve.wait_ge(S["back"], n - 1)
                    own.after(V.tensor_tensor(h[:, n % 2], h[:, n % 2], ps[:, 3 + n % 2, 0:I2], ALU.mult))
                    fp4_steps(nc, own, h[:, n % 2], hq[:, n % 2], ax[:, 0:I2], mag[:, 0:I2],
                              am[:, 0, 0:22], am[:, 1, 0:22], 22).then_inc(S["hq"], 1)
                    dve.wait_ge(S["hq"], n + 1)
                dve.wait_ge(S["projected"], c + 1)
                V.tensor_tensor(src, src, ps[:, 6], ALU.add).then_inc(S["added"], 1)
                dve.wait_ge(S["added"], c + 1)
    if old:
        old.close()


SLOTS = 2 * NE


def route_stage(nc, P, r):
    S, clear, old = P.open("dve act router turned copied logits shifted expd chosen ranked")
    T16 = NTOK // 128
    with ExitStack() as ctx:
        def sb(name, shape, dt=F32):
            return ctx.enter_context(nc.sbuf_tensor(name, shape, dt))
        cur_t = sb("u_curt", [128, 4, 512])
        router = sb("u_router", [128, NE])
        mx = sb("u_mx", [128, 2, T16])
        sh = sb("u_sh", [128, T16, NE])
        eq = sb("u_eq", [128, T16, NE])
        one = sb("u_one", [128, T16, NE])
        tot = sb("u_tot", [128, NE, T16])
        inc = sb("u_inc", [128, NE, T16])
        cnt = sb("u_cnt", [128, 3, NE])
        fin = sb("u_fin", [128, T16])
        cmp_ = sb("u_cmp", [128, SLOTS, NE])
        slot = sb("u_slot", [128, SLOTS])
        block = ctx.enter_context(nc.Block())
        clear_sems(block, clear)
        ps = P.ps
        lg = ps[:, 4, 0:256].rearrange("p (t e) -> p t e", e=NE)

        @block.tensor
        def _(pe):
            for b in range(4):
                for j in range(4):
                    mm = nc.tensor.transpose(ps[:, b, 128 * j:128 * j + 128], P.cur[:, 4 * b + j], P.col("ident"))
                mm.then_inc(S["turned"], 1)
            pe.wait_ge(S["router"], 1)
            for b in range(4):
                pe.wait_ge(S["copied"], b + 1)
                for j in range(4):
                    mm = nc.tensor.matmul(lg[:, 4 * b + j], cur_t[:, b, 128 * j:128 * j + 128], router[:],
                                          start=True, stop=True)
            mm.then_inc(S["logits"], 1)
            pe.wait_ge(S["chosen"], 1)
            flat = one[:].rearrange("p t e -> p (t e)")
            nc.tensor.matmul(ps[:, 5, 0:256], P.col("tri"), flat, start=True, stop=True)
            nc.tensor.matmul(ps[:, 6, 0:256], P.col("ones"), flat, start=True, stop=True)\
                .then_inc(S["ranked"], 1)

        @block.scalar
        def _(act):
            for b in range(4):
                act.wait_ge(S["turned"], b + 1)
                nc.scalar.copy(cur_t[:, b], ps[:, b]).then_inc(S["copied"], 1)
            act.wait_ge(S["shifted"], 1)
            nc.scalar.activation(sh[:], sh[:], ACT.Exp).then_inc(S["expd"], 1)

        @block.vector
        def _(dve):
            own = Steps(dve, S["dve"])
            V = nc.vector

            def by_tile(ap):
                return ap.rearrange("p (t o) -> p t o", o=1).to_broadcast([128, T16, NE])
            V.tensor_copy(router[:], P.col("u_r")[:, bass.ds(r * NE, NE)]).then_inc(S["router"], 1)
            dve.wait_ge(S["logits"], 1)
            own.after(V.tensor_reduce(mx[:, 0], lg, AX.X, ALU.max))
            V.tensor_tensor(sh[:], lg, by_tile(mx[:, 0]), ALU.subtract).then_inc(S["shifted"], 1)
            own.after(V.tensor_tensor(eq[:], lg, by_tile(mx[:, 0]), ALU.is_equal))
            own.after(V.tensor_tensor(eq[:], eq[:], P.col("desc16")[:, None, :].to_broadcast([128, T16, NE]),
                                      ALU.mult))
            own.after(V.tensor_reduce(mx[:, 1], eq[:], AX.X, ALU.max))
            V.tensor_tensor(one[:], eq[:], by_tile(mx[:, 1]), ALU.is_equal).then_inc(S["chosen"], 1)
            dve.wait_ge(S["expd"], 1)
            own.after(V.tensor_reduce(fin[:], sh[:], AX.X, ALU.add))
            own.after(V.reciprocal(P.weight[:], fin[:]))
            dve.wait_ge(S["ranked"], 1)
            own.after(V.tensor_copy(tot[:], ps[:, 6, 0:256].rearrange("p (t e) -> p e t", e=NE)))
            own.after(V.tensor_tensor_scan(inc[:].rearrange("p e t -> p (e t)"), P.col("first"),
                                           tot[:].rearrange("p e t -> p (e t)"), 0.0, ALU.mult, ALU.add))
            own.mark(V.tensor_tensor(tot[:], inc[:], tot[:], ALU.subtract))
            own.after(V.tensor_scalar(cnt[:, 0], inc[:, :, T16 - 1], 1.0 / 128, 127.0 / 128 - 0.5 + 1.0 / 256,
                                      ALU.mult, ALU.add))
            own.after(V.tensor_scalar(cnt[:, 0], cnt[:, 0], ROUND, -ROUND, ALU.add, ALU.add))
            own.after(V.tensor_tensor_scan(cnt[:, 1], P.col("ones")[:, 0:NE], cnt[:, 0], 0.0, ALU.mult, ALU.add))
            own.after(V.tensor_tensor(cnt[:, 2], cnt[:, 1], cnt[:, 0], ALU.subtract))
            own.after(V.tensor_scalar(cnt[:, 2], cnt[:, 2], 128.0, None, ALU.mult))
            own.after(V.tensor_tensor(tot[:], tot[:], cnt[:, 2].rearrange("p (e o) -> p e o", o=1)
                                      .to_broadcast([128, NE, T16]), ALU.add))
            own.after(V.tensor_tensor(eq[:], ps[:, 5, 0:256].rearrange("p (t e) -> p t e", e=NE),
                                      tot[:].rearrange("p e t -> p t e"), ALU.add))
            own.after(V.tensor_tensor(eq[:], eq[:], one[:], ALU.mult))
            own.after(V.tensor_reduce(fin[:], eq[:], AX.X, ALU.add))
            own.mark(V.tensor_copy(P.place[:], fin[:]))
            own.after(V.tensor_tensor(cmp_[:], cnt[:, 1:2].to_broadcast([128, SLOTS, NE]),
                                      P.col("slots").rearrange("p (s o) -> p s o", o=1)
                                      .to_broadcast([128, SLOTS, NE]), ALU.is_le))
            own.after(V.tensor_reduce(slot[:], cmp_[:], AX.X, ALU.add))
            own.after(V.tensor_scalar(slot[:], slot[:], float(NE - 1), None, ALU.min))
            own.after(V.tensor_copy(P.slot_expert[:], slot[:]))
    if old:
        old.close()


def scatter_stage(nc, P, r):
    S, clear, old = P.open("")
    with nc.Block() as block:
        @block.gpsimd
        def _(pool):
            for s in clear:
                pool.sem_clear(s)
            for t in range(NTOK // 128):
                pool.indirect_dma_start(P.sorted_x, bass.IndirectOffsetOnAxis(P.place[:, t:t + 1], 0),
                                        P.cur[:, t], None).then_inc(P.scattered, 16)
            pool.wait_ge(P.scattered, r * (NTOK // 8) + NTOK // 8)
    if old:
        old.close()


def slots_stage(nc, P):
    U = 4
    S, clear, old = P.open("turned x_out hid silued h_turned h_out summed y_out "
                           + " ".join(f"x_in{k} y_dma{k}" for k in range(U)))
    with ExitStack() as ctx:
        def sb(name, shape, dt=F32):
            return ctx.enter_context(nc.sbuf_tensor(name, shape, dt))
        xb = sb("v_x", [128, U, D])
        x_t = sb("v_xt", [128, 2, 128])
        h = sb("v_h", [128, 2, FF])
        h_t = sb("v_ht", [128, 2, FF])
        yb = sb("v_y", [128, U, D])
        block = ctx.enter_context(nc.Block())
        clear_sems(block, clear)
        ps = P.ps
        XT, HB, HT, YB = 0, 2, 4, 6

        def turns(eng, body):
            for k in range(U):
                body(0, k, True)
            with eng.Fori(1, SLOTS // U) as i:
                for k in range(U):
                    body(i, k, False)

        @block.sync
        def _(sp):
            def load(i, k, first):
                if not first:
                    sp.wait_ge(S["turned"], i * U + (k - U + 1))
                sp.dma_start(xb[:, k], P.sorted_x[bass.ds((i * U + k) * 128, 128), :] if not first
                             else P.sorted_x[k * 128:k * 128 + 128, :]).then_inc(S[f"x_in{k}"], 16)
            turns(sp, load)

        @block.tensor
        def _(pe):
            def hidden(i, k, first):
                n1 = i * U + k + 1
                pe.wait_ge(S[f"x_in{k}"], i * 16 + 16)
                if not first or k >= 2:
                    pe.wait_ge(S["x_out"], n1 - 2)
                nc.tensor.transpose(ps[:, XT + k % 2, 0:128], xb[:, k], P.col("ident"))\
                    .then_inc(S["turned"], 1)

            def product1(i, k, first):
                n1 = i * U + k + 1
                e = pe.value_load(P.slot_expert[0:1, bass.ds(i * U + k, 1)] if not first
                                  else P.slot_expert[0:1, k:k + 1], min_val=0, max_val=NE - 1)
                pe.wait_ge(S["x_out"], n1)
                if not first or k >= 2:
                    pe.wait_ge(S["silued"], n1 - 2)
                nc.tensor.matmul(ps[:, HB + k % 2], x_t[:, k % 2],
                                 P.w1_exp[:, bass.ds(e, 1), :].rearrange("p o f -> p (o f)"),
                                 start=True, stop=True).then_inc(S["hid"], 1)

            def turn_hidden(i, k, first):
                n1 = i * U + k + 1
                pe.wait_ge(S["silued"], n1)
                if not first or k >= 2:
                    pe.wait_ge(S["h_out"], n1 - 2)
                for j in range(HC):
                    mm = nc.tensor.transpose(ps[:, HT + k % 2, 128 * j:128 * j + 128],
                                             h[:, k % 2, 128 * j:128 * j + 128], P.col("ident"))
                mm.then_inc(S["h_turned"], 1)

            def product2(i, k, first):
                n1 = i * U + k + 1
                e = pe.value_load(P.slot_expert[0:1, bass.ds(i * U + k, 1)] if not isinstance(i, int)
                                  else P.slot_expert[0:1, i * U + k:i * U + k + 1], min_val=0, max_val=NE - 1)
                pe.wait_ge(S["h_out"], n1)
                if not first or k >= 2:
                    pe.wait_ge(S["y_out"], n1 - 2)
                for j in range(HC):
                    mm = nc.tensor.matmul(ps[:, YB + k % 2, 0:128], h_t[:, k % 2, 128 * j:128 * j + 128],
                                          P.w2_exp[:, bass.ds(e, 1), 128 * j:128 * j + 128]
                                          .rearrange("p o f -> p (o f)"),
                                          start=(j == 0), stop=(j == HC - 1))
                mm.then_inc(S["summed"], 1)

            def step(i, k, first):
                hidden(i, k, first)
                if not (first and k == 0):
                    before = (i, k - 1) if k else (i - 1, U - 1)
                    turn_hidden(*before, first)
                product1(i, k, first)
                if not (first and k == 0):
                    product2(*before, first)
            turns(pe, step)
            turn_hidden(SLOTS // U - 1, U - 1, False)
            product2(SLOTS // U - 1, U - 1, False)

        @block.vector
        def _(dve):
            def x_copy(i, k, first):
                n1 = i * U + k + 1
                dve.wait_ge(S["turned"], n1)
                if not first or k >= 2:
                    dve.wait_ge(S["hid"], n1 - 2)
                nc.vector.tensor_copy(x_t[:, k % 2], ps[:, XT + k % 2, 0:128]).then_inc(S["x_out"], 1)

            def h_copy(i, k, first):
                n1 = i * U + k + 1
                dve.wait_ge(S["h_turned"], n1)
                if not first or k >= 2:
                    dve.wait_ge(S["summed"], n1 - 2)
                nc.vector.tensor_copy(h_t[:, k % 2], ps[:, HT + k % 2]).then_inc(S["h_out"], 1)

            def step(i, k, first):
                x_copy(i, k, first)
                if not (first and k == 0):
                    before = (i, k - 1) if k else (i - 1, U - 1)
                    h_copy(*before, first)
            turns(dve, step)
            h_copy(SLOTS // U - 1, U - 1, False)

        @block.scalar
        def _(act):
            def silu(i, k, first):
                n1 = i * U + k + 1
                act.wait_ge(S["hid"], n1)
                if not first or k >= 2:
                    act.wait_ge(S["h_turned"], n1 - 2)
                nc.scalar.activation(h[:, k % 2], ps[:, HB + k % 2], ACT.Silu).then_inc(S["silued"], 1)

            def store(i, k, first):
                n1 = i * U + k + 1
                act.wait_ge(S["summed"], n1)
                if not first:
                    act.wait_ge(S[f"y_dma{k}"], i * 16)
                nc.scalar.copy(yb[:, k], ps[:, YB + k % 2, 0:128]).then_inc(S["y_out"], 1)
                act.wait_ge(S["y_out"], n1)
                act.dma_start(P.sorted_y[bass.ds((i * U + k) * 128, 128), :] if not isinstance(i, int)
                              else P.sorted_y[(i * U + k) * 128:(i * U + k) * 128 + 128, :],
                              yb[:, k]).then_inc(S[f"y_dma{k}"], 16)

            def step(i, k, first):
                silu(i, k, first)
                if first and k == 0:
                    return
                if k:
                    store(i, k - 1, first)
                else:
                    n1 = i * U
                    act.wait_ge(S["summed"], n1)
                    act.wait_ge(S[f"y_dma{U - 1}"], (i - 1) * 16)
                    nc.scalar.copy(yb[:, U - 1], ps[:, YB + (U - 1) % 2, 0:128]).then_inc(S["y_out"], 1)
                    act.wait_ge(S["y_out"], n1)
                    act.dma_start(P.sorted_y[bass.ds((i * U - 1) * 128, 128), :],
                                  yb[:, U - 1]).then_inc(S[f"y_dma{U - 1}"], 16)
            turns(act, step)
            store(SLOTS // U - 1, U - 1, False)
            for k in range(U):
                act.wait_ge(S[f"y_dma{k}"], 16 * (SLOTS // U))
    if old:
        old.close()


def gather_stage(nc, P, r):
    S, clear, old = P.open("scaled")
    n = NTOK // 128
    with nc.Block() as block:
        @block.gpsimd
        def _(pool):
            for s in clear:
                pool.sem_clear(s)
            for t in range(n):
                pool.indirect_dma_start(P.cur[:, t], None, P.sorted_y,
                                        bass.IndirectOffsetOnAxis(P.place[:, t:t + 1], 0))\
                    .then_inc(P.gathered, 16)

        @block.vector
        def _(dve):
            dve.wait_ge(P.gathered, r * (NTOK // 8) + NTOK // 8)
            nc.vector.tensor_tensor(P.cur[:], P.cur[:], P.weight[:].rearrange("p (t o) -> p t o", o=1)
                                    .to_broadcast([128, n, D]), ALU.mult).then_inc(S["scaled"], 1)
    if old:
        old.close()


def copy_stage(nc, P, first):
    S, clear, old = P.open("moved")
    with nc.Block() as block:
        clear_sems(block, clear)

        @block.vector
        def _(dve):
            dve.wait_ge(P.experts_in, 32)
            if first:
                nc.vector.tensor_copy(P.cur[:], P.x_all[:]).then_inc(S["moved"], 1)
            else:
                nc.vector.tensor_tensor(P.x_all[:], P.x_all[:], P.cur[:], ALU.add).then_inc(S["moved"], 1)

        @block.tensor
        def _(pe):
            pe.wait_ge(P.experts_in, 32)
    if old:
        old.close()


def experts(nc, P):
    with ExitStack() as ctx:
        def sb(name, shape, dt=F32):
            return ctx.enter_context(nc.sbuf_tensor(name, shape, dt))
        P.cur = sb("cur", [128, NTOK // 128, D])
        P.weight = sb("weight", [128, NTOK // 128])
        P.place = sb("place", [128, NTOK // 128], I32)
        P.slot_expert = sb("slot_expert", [128, SLOTS], I32)
        copy_stage(nc, P, True)
        with nc.Fori(0, ROUNDS) as r:
            route_stage(nc, P, r)
            scatter_stage(nc, P, r)
            slots_stage(nc, P)
            gather_stage(nc, P, r)
            sweep_stage(nc, P)
        copy_stage(nc, P, False)
        norm_stage(nc, P, last=True)


def setup_stage(nc, P, io):
    S, clear, old = P.open("dve pool act loaded decay total total_out quant turned copied zeroed stored")
    with ExitStack() as ctx:
        def sb(name, shape, dt=F32):
            return ctx.enter_context(nc.sbuf_tensor(name, shape, dt))
        part = sb("w_part", [128, 4])
        red = sb("w_red", [128, 6])
        fq = sb("w_fq", [128, 3, 384])
        ax = sb("w_ax", [128, 384])
        mag = sb("w_mag", [128, 384])
        am = sb("w_am", [128, 2, 24])
        zero = sb("w_zero", [128, 2048])
        block = ctx.enter_context(nc.Block())

        @block.sync
        def _(sp):
            sp.dma_start(P.w[:], io["cols"]).then_inc(S["loaded"], 16)
            sp.dma_start(P.rows[:], io["rows"]).then_inc(S["loaded"], 16)
            sp.dma_start(P.w1_exp[:], io["w1"]).then_inc(P.experts_in, 16)
            sp.dma_start(P.w2_exp[:], io["w2"]).then_inc(P.experts_in, 16)
            sp.wait_ge(S["zeroed"], 1)
            for half in range(2):
                sp.dma_start(P.sorted_x[half * 2048:half * 2048 + 2048, :].rearrange("(p r) d -> p (r d)", p=128),
                             zero[:]).then_inc(S["stored"], 16)
            sp.wait_ge(S["stored"], 32)

        @block.gpsimd
        def _(pool):
            G = nc.gpsimd
            G.memset(zero[:], 0.0).then_inc(S["zeroed"], 1)
            own = Steps(pool, S["pool"])
            for i, (t, v) in enumerate(((P.v_pairs, 0.0), (P.hpad, 0.0))):
                own.mark(G.memset(t[:], v))
            own.mark(G.memset(P.kpad[:, :, 0:1], FIRST_PP))
            for t in (P.e1b, P.e2b, P.ev):
                own.mark(G.memset(t[:, :, 0:1], 0.0))
            own.wait()
            own.mark(G.memset(P.v_pairs[0:64, :, :, 8:9], 1.0))
            own.after(G.memset(P.v_pairs[64:128, :, :, 17:18], 1.0))

        @block.scalar
        def _(act):
            act.wait_ge(S["loaded"], 32)
            nc.scalar.activation(P.w_dec[:, 1:2], P.col("r_td"), ACT.Exp).then_inc(S["decay"], 1)
            for n in range(3):
                act.wait_ge(S["turned"], n + 1)
                if n < 2:
                    dst = (P.gate_q, P.up_q)[n]
                    nc.scalar.copy(dst[:], P.ps[:, 1 + n, 0:I2]).then_inc(S["copied"], 1)
                else:
                    nc.scalar.copy(P.down_q[:, 0:256], P.ps[:, 3, 0:256]).then_inc(S["copied"], 1)
                    nc.scalar.copy(P.down_q[0:96, 256:384], P.ps[0:96, 3, 256:384]).then_inc(S["copied"], 1)

        @block.tensor
        def _(pe):
            for n in range(2):
                pe.wait_ge(S["total"], n + 1)
                nc.tensor.matmul(P.ps[:, 0, 8 * n:8 * n + 1], P.col("ones"), part[:, n:n + 1],
                                 start=True, stop=True).then_inc(S["total_out"], 1)
            for n in range(3):
                pe.wait_ge(S["quant"], n + 1)
                for j in range(3):
                    w = min(128, I2 - 128 * j)
                    if n < 2:
                        mm = nc.tensor.transpose(P.ps[:, 1 + n, 128 * j:128 * j + w],
                                                 fq[0:w, n, 128 * j:128 * j + 128],
                                                 P.col("ident")[0:w, 0:w])
                    else:
                        mm = nc.tensor.transpose(P.ps[0:w, 3, 128 * j:128 * j + 128],
                                                 fq[:, 2, 128 * j:128 * j + w], P.col("ident"))
                mm.then_inc(S["turned"], 1)

        @block.vector
        def _(dve):
            V = nc.vector
            own = Steps(dve, S["dve"])
            dve.wait_ge(S["loaded"], 32)
            own.mark(V.tensor_copy(P.ident_bf[:], P.col("ident")))
            own.mark(V.tensor_copy(P.causal8[:].rearrange("p (h k) -> p h k", h=8),
                                   P.col("causal")[:, None, :].to_broadcast([128, 8, SEQ])))
            own.mark(V.tensor_copy(P.sel_bf[:], P.col("sel")[0:CSEQ]))
            own.mark(V.tensor_copy(P.spread_bf[:], P.col("spread8")[0:NE8]))
            for j, m in enumerate(("r_mk", "r_mv", "r_mr")):
                own.mark(V.tensor_scalar(P.one_minus[:, j:j + 1], P.col(m), -1.0, 1.0, ALU.mult, ALU.add))
            dve.wait_ge(S["decay"], 1)
            own.mark(V.memset(P.decay[:], 0.0))
            own.after(V.tensor_scalar(P.w_dec[:, 0:1], P.w_dec[:, 1:2], -1.0, None, ALU.mult))
            own.after(V.tensor_scalar(P.decay[:], P.decay[:], P.w_dec[:, 0:1], None, ALU.add))
            own.after(V.memset(P.decay[:, :, 0:1], FIRST_PP))
            for n, (name, dst) in enumerate((("b_w1", P.w1q), ("b_w2", P.w2q))):
                w = P.col(name)
                V.tensor_reduce(part[:, n:n + 1], w, AX.X, ALU.add, apply_absolute_value=True)\
                    .then_inc(S["total"], 1)
                dve.wait_ge(S["total_out"], n + 1)
                m, s = red[:, 3 * n:3 * n + 1], red[:, 3 * n + 1:3 * n + 2]
                own.after(V.tensor_scalar(m, P.ps[:, 0, 8 * n:8 * n + 1], 1.0 / (D * HID1), 1e-5,
                                          ALU.mult, ALU.max))
                own.after(V.reciprocal(s, m))
                inv = red[:, 3 * n + 2:3 * n + 3]
                own.after(V.reciprocal(inv, s))
                own.after(V.tensor_scalar(dst[:], w, s, ROUND, ALU.mult, ALU.add))
                own.after(V.tensor_scalar(dst[:], dst[:], -ROUND, 1.0, ALU.add, ALU.min))
                own.after(V.tensor_scalar(dst[:], dst[:], -1.0, inv, ALU.max, ALU.mult))
            for n, (name, width) in enumerate((("q_g", 384), ("q_u", 384), ("q_d", 352))):
                nb = width // BLK
                fp4_steps(nc, own, P.col(name), fq[:, n, 0:width], ax[:, 0:width], mag[:, 0:width],
                          am[:, 0, 0:nb], am[:, 1, 0:nb], nb).then_inc(S["quant"], 1)
                dve.wait_ge(S["quant"], n + 1)
    if old:
        old.close()


def load_stage(nc, P, io, i):
    S, clear, old = P.open("loaded masked")
    with nc.sbuf_tensor("l_mask", [CSEQ, CHUNKS, SEQ], I32) as mk, nc.Block() as block:
        clear_sems(block, clear)

        @block.sync
        def _(sp):
            sp.dma_start(P.x_tok[:], io["x"].rearrange("(h c t p) d -> h p c t d", h=PASSES, c=CHUNKS, t=TILES)[i])\
                .then_inc(S["loaded"], 16)
            sp.dma_start(P.x_feat[:], io["xt"].rearrange("p (h c t) -> h p c t", h=PASSES, c=CHUNKS)[i])\
                .then_inc(S["loaded"], 16)
            sp.dma_start(P.ctx_feat[:], io["ct"].rearrange("p (h c t) -> h p c t", h=PASSES, c=CHUNKS)[i])\
                .then_inc(S["loaded"], 16)
            sp.dma_start(mk[:], io["mask"].rearrange("(h c s) k -> h s c k", h=PASSES, c=CHUNKS)[i])\
                .then_inc(S["loaded"], 16)
            sp.wait_ge(S["loaded"], 64)

        @block.vector
        def _(dve):
            dve.wait_ge(S["loaded"], 64)
            for c in range(CHUNKS):
                nc.vector.tensor_scalar(P.keys8[:, c].rearrange("p (h k) -> p h k", h=8),
                                        mk[:, c:c + 1, :].to_broadcast([CSEQ, 8, SEQ]), 0.0, NEG,
                                        ALU.is_gt, ALU.mult).then_inc(S["masked"], 1)
    if old:
        old.close()


def keep_stage(nc, P, i):
    S, clear, old = P.open("kept")
    with nc.Block() as block:
        clear_sems(block, clear)

        @block.vector
        def _(dve):
            nc.vector.tensor_copy(P.x_all[:, bass.ds(i * CHUNKS * TILES, CHUNKS * TILES), :],
                                  P.x_tok[:].rearrange("p c t d -> p (c t) d")).then_inc(S["kept"], 1)
    if old:
        old.close()


def sweep_stage(nc, P):
    S, clear, old = P.open("")
    with nc.Block() as block:
        clear_sems(block, clear)
    if old:
        old.close()


def store_stage(nc, P, out):
    S, clear, old = P.open("stored")
    with nc.Block() as block:
        clear_sems(block, clear)

        @block.sync
        def _(sp):
            sp.dma_start(out.rearrange("(t p) d -> p t d", p=128), P.x_all[:]).then_inc(S["stored"], 16)
            sp.wait_ge(S["stored"], 16)
    if old:
        old.close()


def decoder(nc, io, out):
    with ExitStack() as ctx:
        P = Program(nc, ctx)
        P.ps = ctx.enter_context(nc.psum_tensor("ps", [128, 8, 512], F32))
        P.w = P.sb("w", [128, WCOLS])
        P.rows = P.sb("rows", [1, RCOLS])
        P.x_all = P.sb("x_all", [128, NTOK // 128, D])
        P.ident_bf = P.sb("ident_bf", [128, 128], BF16)
        P.causal8 = P.sb("causal8", [128, 512], BF16)
        P.sel_bf = P.sb("sel_bf", [CSEQ, CHUNK], BF16)
        P.spread_bf = P.sb("spread_bf", [NE8, 512], BF16)
        P.sorted_x = nc.dram_tensor("sorted_x", (4096, D), F32).ap()
        P.sorted_y = nc.dram_tensor("sorted_y", (4096, D), F32).ap()
        P.experts_in = ctx.enter_context(nc.semaphore("experts_in"))
        P.scattered = ctx.enter_context(nc.semaphore("scattered"))
        P.gathered = ctx.enter_context(nc.semaphore("gathered"))
        P.w1_exp = P.sb("w1_exp", [128, NE, FF])
        P.w2_exp = P.sb("w2_exp", [128, NE, FF])
        with ExitStack() as loop:
            def lb(name, shape, dt=F32):
                return loop.enter_context(nc.sbuf_tensor(name, shape, dt))
            P.x_tok = lb("x_tok", [128, CHUNKS, TILES, D])
            P.x_feat = lb("x_feat", [128, CHUNKS, CHUNK])
            P.ctx_feat = lb("ctx_feat", [128, CHUNKS, CHUNK])
            P.keys8 = lb("keys8", [CSEQ, CHUNKS, 512], BF16)
            P.v_pairs = lb("v_pairs", [128, CSEQ, 8, 18])
            P.hpad = lb("hpad", [128, 4, CSEQ, SEQ + 2])
            P.kpad = lb("kpad", [128, CSEQ, SEQ + 1])
            P.decay = lb("decay", [128, CSEQ, SEQ + 1])
            P.e1b = lb("e1b", [128, CSEQ, SEQ + 1])
            P.e2b = lb("e2b", [128, CSEQ, SEQ + 1])
            P.ev = lb("ev", [128, CSEQ, SEQ + 1])
            P.w_dec = lb("w_dec", [128, 2])
            P.one_minus = lb("one_minus", [128, 3])
            P.w1q = lb("w1q", [128, HID1])
            P.w2q = lb("w2q", [128, HID1])
            P.gate_q = lb("gate_q", [128, I2])
            P.up_q = lb("up_q", [128, I2])
            P.down_q = lb("down_q", [128, 384])
            setup_stage(nc, P, io)
            stages = [
                lambda: attention_stage(nc, P, "a0q", "a0k", "a0v", P.x_feat, bq="a0bq", bk="a0bk", bv="a0bv",
                                        rope=("a0qs", "a0bqs"), mask="causal",
                                        wo="a0o", bo="a0bo"),
                lambda: quaternion_stage(nc, P),
                lambda: small_experts_stage(nc, P),
                lambda: gated_scan_stage(nc, P),
                lambda: attention_stage(nc, P, "x1q", "x1k", "x1v", P.ctx_feat, bq="x1bq", bk="x1bk",
                                        bv="x1bv", mask="keys"),
                lambda: bitnet_stage(nc, P),
                lambda: rwkv_stage(nc, P),
                lambda: attention_stage(nc, P, "x2q", "x2k", "x2v", P.ctx_feat, kind="sigmoid", wo="x2o"),
                lambda: fp4_stage(nc, P),
                lambda: attention_stage(nc, P, "a3q", "a3k", "a3v", P.x_feat, bq="a3bq", bk="a3bk", bv="a3bv",
                                        mask="causal", wo="a3o", bo="a3bo"),
                lambda: attention_stage(nc, P, "x3q", "x3k", "x3v", P.ctx_feat, relu=True),
            ]
            with nc.Fori(0, PASSES) as i:
                load_stage(nc, P, io, i)
                for stage in stages[:STOP]:
                    stage()
                    norm_stage(nc, P)
                keep_stage(nc, P, i)
                sweep_stage(nc, P)
        if STOP == 11:
            experts(nc, P)
        store_stage(nc, P, out)
        P.old.close()


STOP = 11


def tables():
    f = np.float32
    p = np.arange(128)
    seq, pos = p // SEQ, p % SEQ
    same = (seq[:, None] == seq[None, :])
    T = {}
    T["ident"] = np.eye(128, dtype=f)
    T["ones"] = np.ones((128, 128), f)
    T["head4"] = ((p[:, None] % 32) // HD == np.arange(4)).astype(f)
    half = HD // 2
    theta = (1.0 / np.power(f(10000.0), (np.arange(0, half, 2, dtype=f) / f(half)))).astype(f)
    freq = ((p // HD).astype(f) * theta[((p % HD) % half) // 2]).astype(f)[:, None]
    T["cosr"] = np.cos(freq)
    T["sinr"] = np.sin(freq) * np.where(p % 2 == 0, -1.0, 1.0)[:, None]
    T["causal"] = np.where(np.arange(SEQ)[None, :] > pos[:, None], NEG, 0.0)
    k = np.arange(SEQ)
    filt = np.exp(1j * 1.5 * np.arctan(np.log((k.astype(f) + f(1e-10)).astype(np.float64))))
    full = filt[pos][None, :] * np.exp(-2j * np.pi * pos[:, None] * pos[None, :] / SEQ) * same
    T["dft_c"], T["dft_d"], T["dft_nd"] = full.real, full.imag, -full.imag
    ang = 2 * np.pi * pos[:, None] * pos[None, :] / SEQ
    T["inv_c"] = np.cos(ang) / (2 * SEQ) * same
    T["inv_ns"] = -np.sin(ang) / (2 * SEQ) * same
    sign = np.ones((128, 2, 4, 32))
    sign[:, 0, 2] = -1
    sign[:, 1, 3] = -1
    T["sign"] = sign.reshape(128, 256)
    T["desc8"] = np.broadcast_to(8.0 - np.arange(8), (128, 8))
    T["desc16"] = np.broadcast_to(16.0 - np.arange(16), (128, 16))
    T["spread8"] = (p[:, None] == np.arange(512)[None, :] // FF8)
    n = np.arange(512)
    T["sel"] = (p[:, None] == 2 * (n // 128) + (n % 128) // SEQ)
    T["tri"] = (p[:, None] < p[None, :])
    T["slots"] = np.broadcast_to(np.arange(32.0), (128, 32))
    T["first"] = np.broadcast_to((np.arange(256) % 16 != 0), (128, 256))
    return T


def lay_out(inputs):
    a = {k: np.asarray(v) for k, v in inputs.items()}
    T = tables()
    swap = np.arange(128) ^ 1
    quat = np.concatenate([np.r_[0:32], np.r_[64:96], np.r_[64:96], np.r_[0:32],
                           np.r_[32:64], np.r_[96:128], np.r_[96:128], np.r_[32:64]])

    def tiles(w, n):
        return w.reshape(n, 128, -1).transpose(1, 0, 2).reshape(128, -1)

    def padded(w):
        out = np.zeros((384, 128), w.dtype)
        out[:I2] = w
        return tiles(out, 3)
    rep = np.tile(np.arange(HD), HEADS)
    C = dict(T)
    C["a0q"], C["a0qs"] = a["L0_attn_Wq"], a["L0_attn_Wq"][:, swap]
    C["a0k"] = a["L0_attn_Wk"][:, rep]
    C["a0v"], C["a0o"] = a["L0_attn_Wv"][:, rep], a["L0_attn_Wo"]
    C["a0bq"], C["a0bqs"] = a["L0_attn_bq"][:, None], a["L0_attn_bq"][swap][:, None]
    C["a0bk"] = a["L0_attn_bk"][rep][:, None]
    for n in "qkv":
        C["f_" + n] = a["L0_xattn_w" + n][:, quat]
    C["m_r"] = a["L0_ffn_w_router"].T
    C["m_fc"] = a["L0_ffn_w_fc"].reshape(512, 128).T
    C["m_pj"] = tiles(a["L0_ffn_w_proj"].transpose(0, 2, 1).reshape(512, 128), 4)
    C["g_hg"] = a["L1_attn_W_hg"].T
    for n in "qkv":
        C["x1" + n] = a[f"L1_xattn_{n}_w"].T
    C["x1bq"], C["x1bk"] = a["L1_xattn_q_b"][:, None], a["L1_xattn_k_b"][:, None]
    C["b_w1"] = a["L1_ffn_w1"].T
    C["b_w2"] = tiles(a["L1_ffn_w2"].T, 4)
    C["b_cw"] = tiles(a["L1_ffn_conv_w"].reshape(512, 3), 4)
    C["b_cb"] = tiles(a["L1_ffn_conv_b"].reshape(512, 1), 4)
    for n in "kvro":
        C["r_" + n] = a[f"L2_attn_W{n}"].T
    for n in "kvr":
        C["r_m" + n] = a[f"L2_attn_time_mix_{n}"].reshape(128, 1)
    C["r_td"], C["r_tf"] = a["L2_attn_time_decay"][:, None], a["L2_attn_time_first"][:, None]
    for n in "qkvo":
        C["x2" + n] = a[f"L2_xattn_W{n}"].T
    C["q_g"], C["q_u"], C["q_d"] = padded(a["L2_ffn_w_gate"]), padded(a["L2_ffn_w_up"]), a["L2_ffn_w_down"]
    for n, m in zip("qkvo", "qkvm"):
        C["a3" + n] = a[f"L3_attn_W{m}"]
    C["a3bq"], C["a3bk"] = a["L3_attn_bq"][:, None], a["L3_attn_bk"][:, None]
    for n in "qkv":
        C["x3" + n] = a[f"L3_xattn_W{n}"].T
    C["u_r"] = a["L3_ffn_routers"].transpose(1, 0, 2).reshape(128, -1)
    R = {"ones": np.ones(128, np.float32), "a0bv": a["L0_attn_bv"][rep], "a0bo": a["L0_attn_bo"],
         "x1bv": a["L1_xattn_v_b"], "a3bv": a["L3_attn_bv"], "a3bo": a["L3_attn_bm"]}
    for n in "qkv":
        R["f_b" + n] = a["L0_xattn_b" + n][quat]
    cols = np.empty((128, WCOLS), np.float32)
    for name, (at, width) in COL_AT.items():
        cols[:, at:at + width] = C[name]
    rows = np.empty((1, RCOLS), np.float32)
    for name, (at, width) in ROW_AT.items():
        rows[0, at:at + width] = R[name]
    x = a["x"].reshape(NTOK, D)
    return {
        "cols": cols, "rows": rows, "x": x, "xt": np.ascontiguousarray(x.T),
        "ct": np.ascontiguousarray(a["ctx_1024"].reshape(NTOK, D).T), "mask": a["mask_BxS2_ik0"],
        "w1": np.ascontiguousarray(a["L3_ffn_W1"].transpose(1, 0, 2)),
        "w2": np.ascontiguousarray(a["L3_ffn_W2"].reshape(NE, HC, 128, D).transpose(2, 0, 1, 3)
                                   .reshape(128, NE, FF)),
    }


def kernel(**inputs):
    import concourse.bacc as _bacc
    from concourse.bass_utils import run_bass_kernel_spmd as _run
    nc = _bacc.Bacc("TRN2", target_bir_lowering=False, num_devices=1)
    arrays = {f"in_{k}": v for k, v in lay_out(inputs).items()}
    io = {k[3:]: nc.dram_tensor(k, v.shape, mybir.dt.from_np(v.dtype), kind="ExternalInput").ap()
          for k, v in arrays.items()}
    out = nc.dram_tensor("out", (NTOK, D), F32, kind="ExternalOutput").ap()
    decoder(nc, io, out)
    r = _run(nc, [arrays], core_ids=[0])
    return r.results[0]["out"].reshape(BATCH, SEQ, D)
```
